# Optimizing a Trainium2 kernel written in Bass

```python
import numpy as np
import jax
import jax.numpy as jnp

def _softmax(x, axis=-1):
    return jax.nn.softmax(x, axis=axis)

def _gelu(x):
    return jax.nn.gelu(x, approximate=True)

def _silu(x):
    return jax.nn.silu(x)

def _sigmoid(x):
    return jax.nn.sigmoid(x)

def _layernorm(x, axis=-1, eps=1e-05):
    m = jnp.mean(x, axis=axis, keepdims=True)
    v = jnp.var(x, axis=axis, keepdims=True)
    return (x - m) / jnp.sqrt(v + eps)

def _scatter_add(tgt, idx, src, axis=0):
    return tgt.at[idx].add(src)

def _segment_sum(src, seg, n):
    return jax.ops.segment_sum(src, seg, n)
kernel_name = 'mk_adaln_d1_jaxref_r8_470208'

def setup_inputs(seed: int=0):
    np.random.seed(seed)
    _w = jnp.asarray

    def _L0_attn_setup():
        import jax, jax.numpy as jnp
        import numpy as np
        EPS = 1e-08
        C_RGLRU = 8.0

        def rmsnorm(x, w):
            rms = jnp.sqrt(jnp.mean(x * x, axis=-1, keepdims=True) + EPS)
            return w * (x / rms)

        def causal_depthwise_conv(x, conv_w, conv_b):
            K = conv_w.shape[0]
            S = x.shape[1]
            xp = jnp.pad(x, ((0, 0), (K - 1, 0), (0, 0)))
            y = sum((conv_w[k] * xp[:, k:k + S, :] for k in range(K)))
            return y + conv_b

        def rg_lru(x, ga_W, ga_b, gx_W, gx_b, a_param):
            r = jax.nn.sigmoid(x @ ga_W + ga_b)
            i = jax.nn.sigmoid(x @ gx_W + gx_b)
            log_a = -C_RGLRU * jax.nn.softplus(a_param) * r
            a = jnp.exp(log_a)
            mult = jnp.sqrt(-jnp.expm1(2.0 * log_a))
            b = mult * (i * x)

            def combine(c1, c2):
                a1, b1 = c1
                a2, b2 = c2
                return (a1 * a2, a2 * b1 + b2)
            _, h = jax.lax.associative_scan(combine, (a, b), axis=1)
            return h
        D, H, F, K, B, S = (256, 256, 768, 4, 2, 256)
        key = jax.random.key(seed)
        ks = jax.random.split(key, 16)

        def lin(k, fan_in, shape):
            return jax.random.normal(k, shape, jnp.float32) * fan_in ** (-0.5)
        return {'x': jax.random.normal(ks[0], (B, S, D), jnp.float32), 'norm1_w': jnp.ones((D,), jnp.float32), 'left_W': lin(ks[1], D, (D, H)), 'left_b': jnp.zeros((H,), jnp.float32), 'right_W': lin(ks[2], D, (D, H)), 'right_b': jnp.zeros((H,), jnp.float32), 'conv_w': lin(ks[3], K, (K, H)), 'conv_b': jnp.zeros((H,), jnp.float32), 'ga_W': lin(ks[4], H, (H, H)), 'ga_b': jnp.zeros((H,), jnp.float32), 'gx_W': lin(ks[5], H, (H, H)), 'gx_b': jnp.zeros((H,), jnp.float32), 'a_param': jax.random.uniform(ks[6], (H,), jnp.float32, 0.5, 3.0), 'out_W': lin(ks[7], H, (H, D)), 'out_b': jnp.zeros((D,), jnp.float32), 'norm2_w': jnp.ones((D,), jnp.float32), 'up1_W': lin(ks[8], D, (D, F)), 'up1_b': jnp.zeros((F,), jnp.float32), 'up2_W': lin(ks[9], D, (D, F)), 'up2_b': jnp.zeros((F,), jnp.float32), 'down_W': lin(ks[10], F, (F, D)), 'down_b': jnp.zeros((D,), jnp.float32)}
    _L0_attn_in = _L0_attn_setup()

    def _L0_ffn_setup():
        import jax, jax.numpy as jnp
        import numpy as np
        B, S, H, F, E = (4, 256, 256, 1024, 8)
        TOP_K = 2

        def _moe_forward(hidden_states, gate_w, w1, b1, w2, b2):
            b, s, h = hidden_states.shape
            tokens = hidden_states.reshape(-1, h)
            T = tokens.shape[0]
            router_logits = tokens @ gate_w
            router_probs = jax.nn.softmax(router_logits, axis=-1)
            top_w, top_idx = jax.lax.top_k(router_probs, TOP_K)
            top_w = top_w / jnp.sum(top_w, axis=-1, keepdims=True)
            cw = jnp.zeros((T, E), dtype=tokens.dtype)
            cw = cw.at[jnp.arange(T)[:, None], top_idx].add(top_w)
            combined = jnp.zeros((T, h), dtype=tokens.dtype)
            for e in range(E):
                hmid = jax.nn.gelu(tokens @ w1[e] + b1[e], approximate=False)
                out_e = hmid @ w2[e] + b2[e]
                combined = combined + cw[:, e:e + 1] * out_e
            return combined.reshape(b, s, h) + hidden_states
        key = jax.random.key(seed)
        ks = jax.random.split(key, 7)
        scale = 0.02
        return {'hidden_states': jax.random.normal(ks[0], (B, S, H), dtype=jnp.float32), 'gate_w': jax.random.normal(ks[1], (H, E), dtype=jnp.float32) * scale, 'w1': jax.random.normal(ks[2], (E, H, F), dtype=jnp.float32) * scale, 'b1': jnp.zeros((E, F), dtype=jnp.float32), 'w2': jax.random.normal(ks[3], (E, F, H), dtype=jnp.float32) * scale, 'b2': jnp.zeros((E, H), dtype=jnp.float32)}
    _L0_ffn_in = _L0_ffn_setup()
    _L0_c = _w((lambda *s: np.random.randn(*s).astype(np.float32) * 0.05)(4, 256))
    _L0_wmod = _w((lambda *s: np.random.randn(*s).astype(np.float32) * 0.05)(256, 6 * 256) * 256 ** (-0.5))
    _d = {'L0_attn_x': _L0_attn_in['x'], 'L0_attn_norm1_w': _L0_attn_in['norm1_w'], 'L0_attn_left_W': _L0_attn_in['left_W'], 'L0_attn_left_b': _L0_attn_in['left_b'], 'L0_attn_right_W': _L0_attn_in['right_W'], 'L0_attn_right_b': _L0_attn_in['right_b'], 'L0_attn_conv_w': _L0_attn_in['conv_w'], 'L0_attn_conv_b': _L0_attn_in['conv_b'], 'L0_attn_ga_W': _L0_attn_in['ga_W'], 'L0_attn_ga_b': _L0_attn_in['ga_b'], 'L0_attn_gx_W': _L0_attn_in['gx_W'], 'L0_attn_gx_b': _L0_attn_in['gx_b'], 'L0_attn_a_param': _L0_attn_in['a_param'], 'L0_attn_out_W': _L0_attn_in['out_W'], 'L0_attn_out_b': _L0_attn_in['out_b'], 'L0_attn_norm2_w': _L0_attn_in['norm2_w'], 'L0_attn_up1_W': _L0_attn_in['up1_W'], 'L0_attn_up1_b': _L0_attn_in['up1_b'], 'L0_attn_up2_W': _L0_attn_in['up2_W'], 'L0_attn_up2_b': _L0_attn_in['up2_b'], 'L0_attn_down_W': _L0_attn_in['down_W'], 'L0_attn_down_b': _L0_attn_in['down_b'], 'L0_ffn_gate_w': _L0_ffn_in['gate_w'], 'L0_ffn_w1': _L0_ffn_in['w1'], 'L0_ffn_b1': _L0_ffn_in['b1'], 'L0_ffn_w2': _L0_ffn_in['w2'], 'L0_ffn_b2': _L0_ffn_in['b2'], 'L0_c': _L0_c, 'L0_wmod': _L0_wmod}
    _x0 = _d['L0_attn_x']
    _d['L0_attn_x'] = jax.random.normal(jax.random.fold_in(jax.random.key(seed), 1), (4, 256, 256), dtype=_x0.dtype)
    del _x0
    return _d

def reference(L0_attn_x, L0_attn_norm1_w, L0_attn_left_W, L0_attn_left_b, L0_attn_right_W, L0_attn_right_b, L0_attn_conv_w, L0_attn_conv_b, L0_attn_ga_W, L0_attn_ga_b, L0_attn_gx_W, L0_attn_gx_b, L0_attn_a_param, L0_attn_out_W, L0_attn_out_b, L0_attn_norm2_w, L0_attn_up1_W, L0_attn_up1_b, L0_attn_up2_W, L0_attn_up2_b, L0_attn_down_W, L0_attn_down_b, L0_ffn_gate_w, L0_ffn_w1, L0_ffn_b1, L0_ffn_w2, L0_ffn_b2, L0_c, L0_wmod):

    def _L0_attn_ref(x, norm1_w, left_W, left_b, right_W, right_b, conv_w, conv_b, ga_W, ga_b, gx_W, gx_b, a_param, out_W, out_b, norm2_w, up1_W, up1_b, up2_W, up2_b, down_W, down_b):
        import jax, jax.numpy as jnp
        import numpy as np
        EPS = 1e-08
        C_RGLRU = 8.0

        def rmsnorm(x, w):
            rms = jnp.sqrt(jnp.mean(x * x, axis=-1, keepdims=True) + EPS)
            return w * (x / rms)

        def causal_depthwise_conv(x, conv_w, conv_b):
            K = conv_w.shape[0]
            S = x.shape[1]
            xp = jnp.pad(x, ((0, 0), (K - 1, 0), (0, 0)))
            y = sum((conv_w[k] * xp[:, k:k + S, :] for k in range(K)))
            return y + conv_b

        def rg_lru(x, ga_W, ga_b, gx_W, gx_b, a_param):
            r = jax.nn.sigmoid(x @ ga_W + ga_b)
            i = jax.nn.sigmoid(x @ gx_W + gx_b)
            log_a = -C_RGLRU * jax.nn.softplus(a_param) * r
            a = jnp.exp(log_a)
            mult = jnp.sqrt(-jnp.expm1(2.0 * log_a))
            b = mult * (i * x)

            def combine(c1, c2):
                a1, b1 = c1
                a2, b2 = c2
                return (a1 * a2, a2 * b1 + b2)
            _, h = jax.lax.associative_scan(combine, (a, b), axis=1)
            return h
        gelu = lambda t: jax.nn.gelu(t, approximate=False)
        xn = rmsnorm(x, norm1_w)
        left = gelu(xn @ left_W + left_b)
        right = rg_lru(causal_depthwise_conv(xn @ right_W + right_b, conv_w, conv_b), ga_W, ga_b, gx_W, gx_b, a_param)
        x1 = left * right @ out_W + out_b + x
        x1n = rmsnorm(x1, norm2_w)
        mlp = gelu(x1n @ up1_W + up1_b) * (x1n @ up2_W + up2_b) @ down_W + down_b
        return mlp + x1

    def _L0_ffn_ref(hidden_states, gate_w, w1, b1, w2, b2):
        import jax, jax.numpy as jnp
        import numpy as np
        B, S, H, F, E = (4, 256, 256, 1024, 8)
        TOP_K = 2

        def _moe_forward(hidden_states, gate_w, w1, b1, w2, b2):
            b, s, h = hidden_states.shape
            tokens = hidden_states.reshape(-1, h)
            T = tokens.shape[0]
            router_logits = tokens @ gate_w
            router_probs = jax.nn.softmax(router_logits, axis=-1)
            top_w, top_idx = jax.lax.top_k(router_probs, TOP_K)
            top_w = top_w / jnp.sum(top_w, axis=-1, keepdims=True)
            cw = jnp.zeros((T, E), dtype=tokens.dtype)
            cw = cw.at[jnp.arange(T)[:, None], top_idx].add(top_w)
            combined = jnp.zeros((T, h), dtype=tokens.dtype)
            for e in range(E):
                hmid = jax.nn.gelu(tokens @ w1[e] + b1[e], approximate=False)
                out_e = hmid @ w2[e] + b2[e]
                combined = combined + cw[:, e:e + 1] * out_e
            return combined.reshape(b, s, h) + hidden_states
        return _moe_forward(hidden_states, gate_w, w1, b1, w2, b2)
    x = L0_attn_x
    mod = (_silu(L0_c) @ L0_wmod).reshape(L0_c.shape[0], 6, 1, -1)
    sa, ca, ga, sb, cb, gb = (mod[:, 0], mod[:, 1], mod[:, 2], mod[:, 3], mod[:, 4], mod[:, 5])
    ga = (2 * (ga >= 0) - 1) * jnp.maximum(jnp.abs(ga), 0.25)
    gb = (2 * (gb >= 0) - 1) * jnp.maximum(jnp.abs(gb), 0.25)
    h = _layernorm(x, axis=-1) * (1 + ca) + sa
    x = x + ga * _L0_attn_ref(h, L0_attn_norm1_w, L0_attn_left_W, L0_attn_left_b, L0_attn_right_W, L0_attn_right_b, L0_attn_conv_w, L0_attn_conv_b, L0_attn_ga_W, L0_attn_ga_b, L0_attn_gx_W, L0_attn_gx_b, L0_attn_a_param, L0_attn_out_W, L0_attn_out_b, L0_attn_norm2_w, L0_attn_up1_W, L0_attn_up1_b, L0_attn_up2_W, L0_attn_up2_b, L0_attn_down_W, L0_attn_down_b)
    h = _layernorm(x, axis=-1) * (1 + cb) + sb
    x = x + gb * _L0_ffn_ref(h, L0_ffn_gate_w, L0_ffn_w1, L0_ffn_b1, L0_ffn_w2, L0_ffn_b2)
    return x

_drawn_inputs = setup_inputs


def setup_inputs(seed=0):
    import zlib

    import numpy as np

    out = dict(_drawn_inputs(seed))
    spreads = {'L0_attn_norm1_w': (1.0, 0.2),
     'L0_attn_left_b': (0.0, 0.614),
     'L0_attn_right_b': (0.0, 0.53),
     'L0_attn_conv_b': (0.0, 0.563),
     'L0_attn_ga_b': (0.0, 0.8),
     'L0_attn_gx_b': (0.0, 0.8),
     'L0_attn_out_b': (0.0, 0.1),
     'L0_attn_norm2_w': (1.0, 0.2),
     'L0_attn_up1_b': (0.0, 0.437),
     'L0_attn_up2_b': (0.0, 0.464),
     'L0_attn_down_b': (0.0, 0.335),
     'L0_ffn_b1': (0.0, 0.8),
     'L0_ffn_b2': (0.0, 0.478)}
    factors = {'L0_attn_ga_W': 6.829, 'L0_attn_a_param': 8.0, 'L0_ffn_w1': 3.099, 'L0_ffn_w2': 2.89}
    for name, (base, spread) in spreads.items():
        noise = np.random.default_rng([zlib.crc32(name.encode()), seed]).standard_normal(out[name].shape)
        drawn = base * np.exp(spread * noise) if base else spread * noise
        out[name] = jnp.asarray(drawn.astype(out[name].dtype))
    for name, factor in factors.items():
        out[name] = (out[name] * factor).astype(out[name].dtype)
    return out
```

```python
from contextlib import ExitStack

import concourse.bass as bass
from concourse import mybir

ALU = mybir.AluOpType
ACT = mybir.ActivationFunctionType
F32 = mybir.dt.float32
F32R = mybir.dt.float32r
I32 = mybir.dt.int32

P = 128
HT = 512
CAP = 320


class Order:

    def __init__(self):
        self.filled, self.drained, self.at, self.next = [0] * 8, [0] * 8, {}, 0

    def take(self, key, drains=1, bank=None):
        b = self.next if bank is None else bank
        self.next = (b + 1) % 8
        self.filled[b] += 1
        self.at[key] = (b, self.filled[b], self.drained[b])
        self.drained[b] += drains

    def loop(self, key, bank):
        self.at[key] = (bank, self.filled[bank], self.drained[bank])


class Steps:

    def __init__(self, engine, sem):
        self.engine, self.sem, self.n = engine, sem, 0

    def mark(self, ins):
        ins.then_inc(self.sem, 1)
        self.n += 1
        return self.n

    def need(self, n):
        self.engine.wait_ge(self.sem, n)

    def link(self, ins):
        self.need(self.mark(ins))


def adaln_block(nc, I, out):
    B, S, D = I["L0_attn_x"].shape
    H = I["L0_attn_left_W"].shape[1]
    F = I["L0_attn_up1_W"].shape[1]
    _, E = I["L0_ffn_gate_w"].shape
    FE = I["L0_ffn_w1"].shape[2]
    T = B * S
    NH = T // HT
    TT = T // P
    TH = HT // P
    BH = HT // S
    KD, KH, KF, KE = D // P, H // P, F // P, FE // P
    TAPS = I["L0_attn_conv_w"].shape[0]
    PAD = TAPS - 1
    assert KD == 2 and KH == KD and KF == 6 and NH == 2 and BH == 2 and E == 8 and KE == 8
    EPACK = KD * FE
    assert KE * D == EPACK

    names = [("norm1_w", KD), ("left_b", KH), ("right_b", KH), ("conv_w", TAPS * KH), ("conv_b", KH),
             ("ga_b", KH), ("gx_b", KH), ("a_param", KH), ("out_b", KD), ("norm2_w", KD),
             ("up1_b", KF), ("up2_b", KF), ("down_b", KD)]
    row, NV = {}, 0
    for n, k in names:
        row[n], NV = NV, NV + k

    order = Order()
    for key in ["vec", "cT", "mod", ("xh", 0, 0), ("xh", 0, 1), "b1", ("gb", 0), ("gb", 1), ("ms", 0),
                ("xh", 1, 0), ("xh", 1, 1), ("rb", 0), ("ms", 1)]:
        order.take(key, drains=2 if key[0] in ("xh", "rb") else 1)
    for hf in range(NH):
        for m in range(KH):
            order.take(("right", hf, m), drains=2)
        if hf == 0:
            order.take(("rb", 1), drains=2)
    for hf in range(NH):
        for m in range(KH):
            order.take(("left", hf, m))
    for hf in range(NH):
        for dt in range(KD):
            order.take(("xr", hf, dt))
    for hf in range(NH):
        for m in range(KH):
            for g in range(2):
                order.take(("gate", hf, m, g))
    for hf in range(NH):
        for dt in range(KD):
            order.take(("out", hf, dt))
    for hf in range(NH):
        order.take(("ms2", hf))
        order.take(("rb2", hf), drains=2)
    for hf in range(NH):
        for m in range(KF):
            order.take(("up1", hf, m))
            order.take(("up2", hf, m))
    for hf in range(NH):
        for dt in range(KD):
            order.take(("down", hf, dt))
    for hf in range(NH):
        for p in range(2):
            order.take(("x2t", hf, p), drains=2)
        for dt in range(KD):
            order.take(("xh2", hf, dt), drains=2)
    order.take("logits", drains=2)
    for p in range(TT // 2):
        order.take(("h2t", p))
    order.take("places")
    order.take("cwT0")
    order.take("cwT1")
    for p in range(TT // 2):
        order.take(("b2", p))
    for j in range(4):
        order.loop(("s1", j), j)
        order.loop(("rest", j), 4 + j)

    ctx = ExitStack()
    with ctx:
        sem = lambda n: ctx.enter_context(nc.semaphore(n))
        bank = [ctx.enter_context(nc.psum_tensor(f"bank{b}", [P, HT], F32)) for b in range(8)]
        filled = [sem(f"bank_filled{b}") for b in range(8)]
        drained = [sem(f"bank_drained{b}") for b in range(8)]

        top = [(nc.sbuf_base + 31) // 32 * 32]

        def at(name, off, shape, dt=F32):
            return nc.alloc_sbuf_tensor_at(name, [P, *shape], dt, offset=off)

        def region(size):
            off = top[0]
            top[0] += (size + 31) // 32 * 32
            return off

        def new(name, shape, dt=F32):
            n = 4
            for s in shape:
                n *= s
            return at(name, region(n), shape, dt)

        ident = new("ident", [P])
        rows = new("rows", [P])
        rows_e = new("rows_e", [P])
        cols = new("cols", [NV])
        b1c = new("b1c", [E * KE])
        b1_now = new("b1_now", [KE])
        mod = new("mod", [12, B])
        gbb = new("gbb", [B, D])
        small = new("small", [64])
        c_row = new("c_row", [D])
        cT = new("cT", [KD, B])
        gate_w = new("gate_w", [KD, E])
        b2_row = new("b2_row", [D])
        stat = new("stat", [TT, 6])
        mv = new("mv", [TT, 2])
        std = new("std", [TT])
        rstd = new("rstd", [TT])
        rms = new("rms", [2, TH])
        rinv = new("rinv", [2, TH])
        before = new("before", [E, E])
        earlier = new("earlier", [P])
        all_ones = new("all_ones", [P])
        slot_base = new("slot_base", [E])
        overflow = new("overflow", [1], I32)
        slot_a, slot_b = new("slot_a", [TT], I32), new("slot_b", [TT], I32)
        b1_own = new("b1_own", [2, KE])
        w_a, w_b = new("w_a", [TT]), new("w_b", [TT])
        lru = new("lru", [8, KH])
        rt = new("rt", [9, TT, E])
        o_xT = top[0]
        xT = new("xT", [KD, T])
        hT = new("hT", [KD, T])
        o_n = top[0]
        n_hi = new("n_hi", [KD, T], F32R)
        n_lo = new("n_lo", [KD, T], F32R)
        EB = EPACK * 4
        first = [("right", H), ("left", H), ("ga", H), ("gx", H), ("out", D)]
        NA = len(first) * KD * D
        o_wa = top[0]
        wa_hi, wa_lo = new("wa_hi", [len(first), KD, D], F32R), new("wa_lo", [len(first), KD, D], F32R)
        NM = KD * F
        second = ["up1", "up2", "down"]
        o_wm = top[0]
        wm_hi, wm_lo = new("wm_hi", [3, NM], F32R), new("wm_lo", [3, NM], F32R)
        o_raw = region(3 * NM * 4)
        raw_a = at("raw_a", o_raw, [len(first), KD, D])
        raw_m = at("raw_m", o_raw, [3, NM])
        o_x = region(TT * D * 4)
        x_tok, x2_tok = at("x_tok", o_x, [TT, D]), at("x2_tok", o_x, [TT, D])
        o_r1 = region(2 * KF * T * 4)
        TB = KD * T * 4
        u = at("u", o_r1, [KH, T])
        square = at("square", o_r1, [KD, T])
        xn = at("xn", o_r1 + TB, [KD, T])
        gel = at("gel", o_r1 + TB, [KH, T])
        u_hi, u_lo = at("u_hi", o_r1 + 2 * TB, [KH, T], F32R), at("u_lo", o_r1 + 3 * TB, [KH, T], F32R)
        y_hi, y_lo = at("y_hi", o_r1 + 4 * TB, [KH, T], F32R), at("y_lo", o_r1 + 5 * TB, [KH, T], F32R)
        v_hi, v_lo = at("v_hi", o_r1, [KF, T], F32R), at("v_lo", o_r1 + 3 * TB, [KF, T], F32R)
        HB = HT * 4
        o_t = region(12 * HB)
        tmp = at("tmp", o_t, [12, HT])
        wmod = at("wmod", o_t, [KD, 6 * D])
        xhat = at("xhat", o_t + 6 * HB, [TT, D])
        o_rbuf = top[0]
        rbuf = new("rbuf", [4, BH, S + PAD])
        e_raw1 = at("e_raw1", o_raw, [EPACK])
        e_raw2 = at("e_raw2", o_raw + EB, [EPACK])
        assert 4 * EB <= 6 * NM * 4 and 2 * EB <= 3 * NM * 4
        e1_hi, e1_lo = at("e1_hi", o_wm, [KD, FE], F32R), at("e1_lo", o_wm + EB, [KD, FE], F32R)
        e2_hi, e2_lo = at("e2_hi", o_wm + 2 * EB, [KE, D], F32R), at("e2_lo", o_wm + 3 * EB, [KE, D], F32R)
        cwT = at("cwT", o_r1 + 3 * TB, [T])
        xhat2 = at("xhat2", o_t, [TT, D])
        g_hi = at("g_hi", o_r1, [KE, T], F32R)
        g_lo = at("g_lo", o_r1 + KE * T * 4, [KE, T], F32R)
        g_raw = at("g_raw", o_r1 + 2 * KE * T * 4, [4, HT])
        acc = at("acc", o_xT, [TT, D])
        assert 2 * KE * T * 4 + 4 * HB <= 2 * KF * T * 4 + 12 * HB
        w1_hi, w1_lo, w2_hi, w2_lo = [], [], [], []
        for s, o in enumerate((o_wa, o_wm)):
            w1_hi.append(at(f"w1_hi{s}", o, [KD, FE], F32R))
            w1_lo.append(at(f"w1_lo{s}", o + EB, [KD, FE], F32R))
        for s, o in enumerate((o_n, o_wm + 2 * EB)):
            w2_hi.append(at(f"w2_hi{s}", o, [KE, D], F32R))
            w2_lo.append(at(f"w2_lo{s}", o + EB, [KE, D], F32R))
        assert 2 * EB <= 2 * NA * 4 and 4 * EB <= 6 * NM * 4 and 2 * EB <= 2 * TB
        h2_tok = at("h2_tok", o_r1, [TT, D])
        y_a, y_b = at("y_a", o_r1 + TB, [TT, D]), at("y_b", o_r1 + 2 * TB, [TT, D])
        CB4 = CAP * 4
        own_hi = at("own_hi", o_r1 + 3 * TB, [KE, CAP], F32R)
        own_lo = at("own_lo", o_r1 + 3 * TB + KE * CB4, [KE, CAP], F32R)
        assert 3 * TB + 2 * KE * CB4 <= 2 * KF * T * 4
        ST = (CAP + P - 1) // P
        LAST = CAP - (ST - 1) * P
        own_raw = at("own_raw", o_t, [4, CAP])
        o_c = o_t + 4 * CB4
        xe_hi = [at(f"xe_hi{s}", o_c + 2 * s * CB4, [KD, CAP], F32R) for s in range(2)]
        xe_lo = [at(f"xe_lo{s}", o_c + (4 + 2 * s) * CB4, [KD, CAP], F32R) for s in range(2)]
        xe_tok = [at(f"xe_tok{s}", o_c + 8 * CB4 + s * ST * D * 4, [ST, D]) for s in range(2)]
        assert 12 * CB4 + 2 * ST * D * 4 <= 12 * HB and 2 * ST * D * 4 <= 4 * BH * (S + PAD) * 4
        y_tok = [at(f"y_tok{s}", o_rbuf + s * ST * D * 4, [ST, D]) for s in range(2)]
        assert top[0] <= nc.sbuf_usable_end, (top[0], nc.sbuf_usable_end)
        ones = small[:, 0:1]
        eps_ln, eps_rms = small[:, 1:2], small[:, 2:3]

        def C(name, k=0):
            return cols[:, row[name] + k:row[name] + k + 1]

        def M(which, dt, b):
            return mod[:, 2 * which + dt, b:b + 1]
        SA, CA, GA, SB, CB, GB = range(6)

        x_view = I["L0_attn_x"].rearrange("b s d -> (b s) d").rearrange("(t p) d -> p t d", p=P)
        out_view = out.rearrange("b s d -> (b s) d").rearrange("(t p) d -> p t d", p=P)

        def packed(w):
            return w.rearrange("(k p) n -> p k n", p=P)

        x_in = [sem(f"x_in{h}") for h in range(NH)]
        vec_in, c_in, wmod_in, ffn_in = sem("vec_in"), sem("c_in"), sem("wmod_in"), sem("ffn_in")
        a_in = [sem(f"a_in_{n}") for n, _ in first]
        m_in = [sem(f"m_in_{n}") for n in second]
        wa_hi_done, wa_lo_done, wm_hi_done, wm_lo_done = (sem(n) for n in ("wa_hi_done", "wa_lo_done", "wm_hi_done", "wm_lo_done"))
        ident_done, consts_done = sem("ident_done"), sem("consts_done")
        silu_done, cT_done, mod_done = sem("silu_done"), sem("cT_done"), sem("mod_done")
        cols_done, gbb_done, lru_done, b1c_done = sem("cols_done"), sem("gbb_done"), sem("lru_done"), sem("b1c_done")
        mv_done, std_done, xhat_done = sem("mv_done"), sem("std_done"), sem("xhat_done")
        h_done, square_done, ms_root, rinv_done = sem("h_done"), sem("square_done"), sem("ms_root"), sem("rinv_done")
        xn_done, n_hi_done, n_lo_done = sem("xn_done"), sem("n_hi_done"), sem("n_lo_done")
        pads_done = sem("pads_done")
        conv_in, conv_done, u_hi_done, u_lo_done = sem("conv_in"), sem("conv_done"), sem("u_hi_done"), sem("u_lo_done")
        xT_done = sem("xT_done")
        gates_out, lru_out, root_out = sem("gates_out"), sem("lru_out"), sem("root_out")
        scan_done = sem("scan_done")
        gelu_done, y_done, y_hi_done, y_lo_done = sem("gelu_done"), sem("y_done"), sem("y_hi_done"), sem("y_lo_done")
        out_used = sem("out_used")
        up_gelu, v_done, v_hi_done, v_lo_done = sem("up_gelu"), sem("v_done"), sem("v_hi_done"), sem("v_lo_done")
        x2_done, x2tok_done = sem("x2_done"), sem("x2tok_done")
        h2_done, h2_hi, h2_lo = sem("h2_done"), sem("h2_hi"), sem("h2_lo")
        top_done, exp_done, cwT_done = sem("top_done"), sem("exp_done"), sem("cwT_done")
        consts2_done, sel_done = sem("consts2_done"), sem("sel_done")
        h2_tok_done, overflow_done, slots_done = sem("h2_tok_done"), sem("overflow_done"), sem("slots_done")
        rest_done, weights_done = sem("rest_done"), sem("weights_done")
        rows_filled, a_scattered, b_scattered = sem("rows_filled"), sem("a_scattered"), sem("b_scattered")
        xe_in = [sem(f"xe_in{s}") for s in range(2)]
        xe_hi_done, xe_lo_done = sem("xe_hi_done"), sem("xe_lo_done")
        own_done, own_hi_done, own_lo_done = sem("own_done"), sem("own_hi_done"), sem("own_lo_done")
        y_made = sem("y_made")
        y_out = [sem(f"y_out{s}") for s in range(2)]
        a_gathered = [sem(f"a_gathered{t}") for t in range(TT)]
        b_gathered = [sem(f"b_gathered{t}") for t in range(TT)]
        w1_hi_done, w1_lo_done, w2_hi_done, w2_lo_done = sem("w1_hi_done"), sem("w1_lo_done"), sem("w2_hi_done"), sem("w2_lo_done")
        raw1_in, raw2_in = sem("raw1_in"), sem("raw2_in")
        e1_hi_done, e1_lo_done = sem("e1_hi_done"), sem("e1_lo_done")
        e2_hi_done, e2_lo_done = sem("e2_hi_done"), sem("e2_lo_done")
        e1_used, e2_used = sem("e1_used"), sem("e2_used")
        eg_done, eg_hi_done, eg_lo_done = sem("eg_done"), sem("eg_hi_done"), sem("eg_lo_done")
        s2_pass, stored = sem("s2_pass"), sem("stored")
        pe_step, act_step, dve_step, pool_step = sem("pe_step"), sem("act_step"), sem("dve_step"), sem("pool_step")
        acc_done = sem("acc_done")
        g_free, acc_turn = sem("g_free"), sem("acc_turn")
        bias_done = sem("bias_done")
        abs_done, x2_half = sem("abs_done"), sem("x2_half")

        def three(m, n):
            return ((m[0], n[0]), (m[0], n[1]), (m[1], n[0]))

        x_rows = nc.dram_tensor("x_rows", (E * CAP, D), F32, kind="Internal").ap()
        y_rows = nc.dram_tensor("y_rows", (E * CAP, D), F32, kind="Internal").ap()
        whole = (ST - 1) * P
        fills = (E * CAP + T - 1) // T

        def overflowed(engine):
            engine.wait_ge(overflow_done, 1)
            return engine.value_load(overflow[0:1, 0:1], min_val=0, max_val=1)

        block = ctx.enter_context(nc.Block())

        @block.sync
        def _(sp):
            for hf in range(NH):
                sp.dma_start(x_tok[:, hf * TH:(hf + 1) * TH, :], x_view[:, hf * TH:(hf + 1) * TH, :]).then_inc(x_in[hf], 16)
                if hf == 0:
                    sp.dma_start(c_row[0:B, :], I["L0_c"]).then_inc(c_in, 16)
                    sp.dma_start(wmod[:, :, 0:2 * D], packed(I["L0_wmod"])[:, :, 0:2 * D]).then_inc(wmod_in, 16)
            def load_a(n):
                sp.dma_start(raw_a[:, n], packed(I["L0_attn_" + first[n][0] + "_W"])).then_inc(a_in[n], 16)

            def load_m(n):
                sp.dma_start(raw_m[:, n].rearrange("p (k n) -> p k n", k=KF if second[n] == "down" else KD),
                             packed(I["L0_attn_" + second[n] + "_W"])).then_inc(m_in[n], 16)
            for n in range(4):
                load_a(n)
            sp.dma_start(wmod[:, :, 2 * D:], packed(I["L0_wmod"])[:, :, 2 * D:]).then_inc(wmod_in, 16)
            load_a(4)
            load_m(2)
            sp.wait_ge(wa_hi_done, len(first))
            sp.wait_ge(wa_lo_done, len(first))
            load_m(0)
            load_m(1)
            sp.wait_ge(wm_hi_done, 3)
            sp.wait_ge(wm_lo_done, 3)
            w1v = I["L0_ffn_w1"].rearrange("e (k p) n -> p e k n", p=P)
            w2v = I["L0_ffn_w2"].rearrange("e (k p) n -> p e k n", p=P)

            def load_w1(e):
                sp.dma_start(e_raw1[:].rearrange("p (e k n) -> p e k n", e=1, k=KD), w1v[:, bass.ds(e, 1)]).then_inc(raw1_in, 16)

            def load_w2(e):
                sp.dma_start(e_raw2[:].rearrange("p (e k n) -> p e k n", e=1, k=KE), w2v[:, bass.ds(e, 1)]).then_inc(raw2_in, 16)
            load_w1(0)
            load_w2(0)
            xr = I["L0_attn_x"].rearrange("b s d -> (b s) d")
            for first_row in range(0, E * CAP, T):
                n = min(T, E * CAP - first_row)
                sp.dma_start(x_rows[first_row:first_row + n], xr[0:n]).then_inc(rows_filled, 16)
            sp.wait_ge(rows_filled, 16 * fills)
            ov = overflowed(sp)
            with sp.If(ov == 0):
                def rows_of(buf, e):
                    r = buf.rearrange("(e c) d -> e c d", c=CAP)[bass.ds(e, 1)]
                    return (r[:, 0:whole].rearrange("e (k p) d -> p (e k) d", p=P), r[:, whole:].rearrange("e c d -> c e d"))

                def load_x(e, s):
                    a, b = rows_of(x_rows, e)
                    sp.dma_start(xe_tok[s][:, 0:ST - 1, :], a).then_inc(xe_in[s], 16)
                    sp.dma_start(xe_tok[s][0:LAST, ST - 1:ST, :], b).then_inc(xe_in[s], 16)

                def expert(i, s, to_come):
                    kept = (lambda v: v) if isinstance(i, int) else sp.snap
                    _, f5, _ = order.at[("rest", 1)]
                    e = kept(i * 2 + s)
                    ahead, turned, ahead2 = kept(i * 2 + s + 1), kept(i * 2 + (s + f5)), kept(i * 2 + s + 2)
                    if to_come >= 1:
                        if s == 0:
                            sp.wait_ge(b_scattered, 16 * TT)
                        sp.wait_ge(filled[5], turned)
                        load_x(ahead, 1 - s)
                    if to_come >= 2:
                        sp.wait_ge(w1_lo_done, ahead2)
                        load_w1(ahead2)
                        sp.wait_ge(w2_lo_done, ahead2)
                        load_w2(ahead2)
                    a, b = rows_of(y_rows, e)
                    sp.wait_ge(y_made, ahead)
                    sp.dma_start(a, y_tok[s][:, 0:ST - 1, :]).then_inc(y_out[s], 16)
                    sp.dma_start(b, y_tok[s][0:LAST, ST - 1:ST, :]).then_inc(y_out[s], 16)
                sp.wait_ge(w1_lo_done, 1)
                load_w1(1)
                sp.wait_ge(a_scattered, 16 * TT)
                load_x(0, 0)
                sp.wait_ge(w2_lo_done, 1)
                load_w2(1)
                with sp.Fori(0, E // 2 - 1) as i:
                    expert(i, 0, 2)
                    expert(i, 1, 2)
                expert(E // 2 - 1, 0, 1)
                expert(E // 2 - 1, 1, 0)
                for p in range(TT // 2):
                    sp.wait_ge(acc_done, 2 * (p + 1))
                    sp.dma_start(out_view[:, 2 * p:2 * p + 2, :], y_b[:, 2 * p:2 * p + 2, :]).then_inc(stored, 16)
                sp.wait_ge(stored, 16 * (TT // 2))
            with sp.Else():
                sp.wait_ge(w1_lo_done, 1)
                sp.wait_ge(w2_lo_done, 1)
                load_w1(0)
                load_w2(0)
                with sp.Fori(1, E) as e:
                    sp.wait_ge(e1_hi_done, e)
                    sp.wait_ge(e1_lo_done, e)
                    load_w1(e)
                    sp.wait_ge(e2_hi_done, e)
                    sp.wait_ge(e2_lo_done, e)
                    load_w2(e)
                for hf in range(NH):
                    sp.wait_ge(acc_done, (hf + 1) * TH)
                    sp.dma_start(out_view[:, hf * TH:(hf + 1) * TH, :], acc[:, hf * TH:(hf + 1) * TH, :]).then_inc(stored, 16)
                sp.wait_ge(stored, 16 * NH)

        @block.tensor
        def _(pe):
            def begin(key):
                b, _, need = order.at[key]
                if need:
                    pe.wait_ge(drained[b], need)
                return b, bank[b]

            def end(ins, b):
                ins.then_inc(filled[b], 1)

            def until_drained(key, times=1):
                b, _, before_ = order.at[key]
                pe.wait_ge(drained[b], before_ + times)

            def transposes(key, src, n, rows_, step=P):
                b, ps = begin(key)
                for j in range(n):
                    ins = nc.tensor.transpose(ps[:, j * step:j * step + rows_], src(j), ident[0:rows_, 0:rows_])
                end(ins, b)

            def product(key, w, x, k, n=HT):
                b, ps = begin(key)
                for c in range(k):
                    for t, (l, r) in enumerate(three(w(c), x(c))):
                        ins = nc.tensor.matmul(ps[:, 0:n], l, r, start=(c == 0 and t == 0), stop=(c == k - 1 and t == 2))
                end(ins, b)
                return ins

            def mean_square(key, hf):
                b, ps = begin(key)
                for j in range(TH):
                    for dt in range(KD):
                        ins = nc.tensor.matmul(ps[:, j:j + 1], square[:, dt, hf * HT + j * P:hf * HT + (j + 1) * P], ones,
                                               start=(dt == 0), stop=(dt == KD - 1))
                end(ins, b)

            def spread(key, hf):
                b, ps = begin(key)
                for j in range(TH):
                    ins = nc.tensor.matmul(ps[:, j * P:(j + 1) * P], rinv[:, hf, j:j + 1].to_broadcast([P, P]), ident[:],
                                           start=True, stop=True)
                end(ins, b)

            hs = [slice(h * HT, (h + 1) * HT) for h in range(NH)]
            pe.wait_ge(ident_done, 2)
            pe.wait_ge(vec_in, 16 * (len(names)))
            transposes("vec", lambda j: rows[0:NV, :], 1, NV)
            pe.wait_ge(silu_done, 1)
            transposes("cT", lambda j: c_row[0:B, j * P:(j + 1) * P], KD, B, step=B)
            until_drained("cT")
            pe.wait_ge(wmod_in, 32)
            b, ps = begin("mod")
            for j in range(12):
                for k in range(KD):
                    ins = nc.tensor.matmul(ps[:, j * B:(j + 1) * B], wmod[:, k, j * P:(j + 1) * P], cT[:, k, :],
                                           start=(k == 0), stop=(k == KD - 1))
            end(ins, b)

            def x_blocks(key, hf, src):
                for dt in range(KD):
                    transposes((key, hf, dt), lambda j: src[:, hf * TH + j, dt * P:(dt + 1) * P], TH, P)
            pe.wait_ge(xhat_done, 1)
            x_blocks("xh", 0, xhat)
            pe.wait_ge(ffn_in, 16 * 3)
            transposes("b1", lambda j: rows_e[0:E * KE, :], 1, E * KE)
            for g in range(2):
                b, ps = begin(("gb", g))
                for bb in range(2):
                    for k in range(KD):
                        ins = nc.tensor.matmul(ps[:, bb * D:(bb + 1) * D], cT[:, k, 2 * g + bb:2 * g + bb + 1].to_broadcast([P, P]),
                                               wmod[:, k, 5 * D:6 * D], start=(k == 0), stop=(k == KD - 1))
                end(ins, b)
            pe.wait_ge(consts_done, 2)
            pe.wait_ge(square_done, KD)
            mean_square(("ms", 0), 0)
            pe.wait_ge(xhat_done, 2)
            x_blocks("xh", 1, xhat)
            pe.wait_ge(rinv_done, 1)
            spread(("rb", 0), 0)
            pe.wait_ge(square_done, 2 * KD)
            mean_square(("ms", 1), 1)

            def wa(n):
                return lambda m: lambda c: (wa_hi[:, n, c, m * P:(m + 1) * P], wa_lo[:, n, c, m * P:(m + 1) * P])

            def wm(n, k):
                w = [x[:, n].rearrange("p (k n) -> p k n", k=k) for x in (wm_hi, wm_lo)]
                return lambda m: lambda c: tuple(x[:, c, m * P:(m + 1) * P] for x in w)

            def split_of(hi, lo, hf):
                return lambda c: (hi[:, c, hs[hf]], lo[:, c, hs[hf]])

            def wa_ready(n):
                pe.wait_ge(wa_hi_done, n + 1)
                pe.wait_ge(wa_lo_done, n + 1)

            def wm_ready(n):
                pe.wait_ge(wm_hi_done, n)
                pe.wait_ge(wm_lo_done, n)

            wa_ready(0)
            for hf in range(NH):
                pe.wait_ge(n_hi_done, KD * (hf + 1))
                pe.wait_ge(n_lo_done, KD * (hf + 1))
                for m in range(KH):
                    product(("right", hf, m), wa(0)(m), split_of(n_hi, n_lo, hf), KD)
                if hf == 0:
                    pe.wait_ge(rinv_done, 2)
                    spread(("rb", 1), 1)
            wa_ready(1)
            for hf in range(NH):
                for m in range(KH):
                    product(("left", hf, m), wa(1)(m), split_of(n_hi, n_lo, hf), KD)
            for hf in range(NH):
                x_blocks("xr", hf, x_tok)
            wa_ready(3)
            for hf in range(NH):
                pe.wait_ge(u_hi_done, KH * (hf + 1))
                pe.wait_ge(u_lo_done, KH * (hf + 1))
                for m in range(KH):
                    for g in range(2):
                        product(("gate", hf, m, g), wa(2 + g)(m), split_of(u_hi, u_lo, hf), KH)
            wa_ready(4)
            for hf in range(NH):
                pe.wait_ge(y_hi_done, KH * (hf + 1))
                pe.wait_ge(y_lo_done, KH * (hf + 1))
                for dt in range(KD):
                    product(("out", hf, dt), wa(4)(dt), split_of(y_hi, y_lo, hf), KH)
            for hf in range(NH):
                pe.wait_ge(square_done, (hf + 3) * KD)
                mean_square(("ms2", hf), hf)
                pe.wait_ge(rinv_done, hf + 3)
                spread(("rb2", hf), hf)
            wm_ready(3)
            for hf in range(NH):
                pe.wait_ge(n_hi_done, KD * (hf + 3))
                pe.wait_ge(n_lo_done, KD * (hf + 3))
                for m in range(KF):
                    product(("up1", hf, m), wm(0, KD)(m), split_of(n_hi, n_lo, hf), KD)
                    product(("up2", hf, m), wm(1, KD)(m), split_of(n_hi, n_lo, hf), KD)
            for hf in range(NH):
                pe.wait_ge(v_hi_done, KF * (hf + 1))
                pe.wait_ge(v_lo_done, KF * (hf + 1))
                for dt in range(KD):
                    product(("down", hf, dt), wm(2, KF)(dt), split_of(v_hi, v_lo, hf), KF)
            for hf in range(NH):
                pe.wait_ge(x2_done, KD * (hf + 1))
                for p in range(2):
                    b, ps = begin(("x2t", hf, p))
                    for q in range(2):
                        for dt in range(KD):
                            t = hf * TH + 2 * p + q
                            ins = nc.tensor.transpose(ps[:, q * D + dt * P:q * D + (dt + 1) * P], xT[:, dt, t * P:(t + 1) * P], ident[:])
                    end(ins, b)
            for hf in range(NH):
                pe.wait_ge(xhat_done, hf + 3)
                x_blocks("xh2", hf, xhat2)
            for dt in range(KD):
                until_drained(("xh2", 1, dt), 2)
            b, ps = begin("logits")
            for t in range(TT):
                for dt in range(KD):
                    ins = nc.tensor.matmul(ps[:, t * E:(t + 1) * E], hT[:, dt, t * P:(t + 1) * P], gate_w[:, dt, :],
                                           start=(dt == 0), stop=(dt == KD - 1))
            end(ins, b)
            for p in range(TT // 2):
                b, ps = begin(("h2t", p))
                for q in range(2):
                    for dt in range(KD):
                        t = 2 * p + q
                        ins = nc.tensor.transpose(ps[:, q * D + dt * P:q * D + (dt + 1) * P], hT[:, dt, t * P:(t + 1) * P], ident[:])
                end(ins, b)
            pe.wait_ge(consts2_done, 3)
            pe.wait_ge(sel_done, 1)
            sel = rt[:, 6, :, :]
            b, ps = begin("places")
            nc.tensor.matmul(ps[:, 0:TT * E], earlier[:], sel.rearrange("p t e -> p (t e)"), start=True, stop=False)
            nc.tensor.matmul(ps[:, TT * E:(TT + 1) * E], all_ones[:], sel[:, 0, :], start=False, stop=False)
            for t in range(TT):
                first_t = max(t + 1, 1)
                n = TT - first_t + (1 if t > 0 else 0)
                if n:
                    ins = nc.tensor.matmul(ps[:, first_t * E:(first_t + n) * E].rearrange("p (t e) -> p t e", e=E), all_ones[:],
                                           sel[:, t:t + 1, :].to_broadcast([P, n, E]), start=False, stop=(t == TT - 1))
            end(ins, b)
            pe.wait_ge(top_done, 1)
            for g in range(2):
                b, ps = begin(f"cwT{g}")
                for j in range(TH):
                    ins = nc.tensor.transpose(ps[0:E, j * P:(j + 1) * P], rt[:, 5, g * TH + j, :], ident[:])
                end(ins, b)
            until_drained("cwT0")
            until_drained("cwT1")
            for p in range(TT // 2):
                b, ps = begin(("b2", p))
                for q in range(2):
                    t = 2 * p + q
                    ins = nc.tensor.matmul(ps[:, q * D:(q + 1) * D], cwT[0:E, t * P:(t + 1) * P], b2_row[0:E, :], start=True, stop=True)
                end(ins, b)

            def all_experts():
                pe.wait_ge(h2_hi, NH * KD)
                pe.wait_ge(h2_lo, NH * KD)
                with pe.Fori(0, E) as e:
                    pe.wait_ge(e1_hi_done, e + 1)
                    pe.wait_ge(e1_lo_done, e + 1)
                    for n in range(NH * KE):
                        hf, f = n // KE, n % KE
                        b, _, need = order.at[("s1", n % 4)]
                        pe.wait_ge(drained[b], e * (NH * KE // 4) + need + n // 4)
                        for c in range(KD):
                            for t, (l, r) in enumerate(three([x[:, c, f * P:(f + 1) * P] for x in (e1_hi, e1_lo)], split_of(n_hi, n_lo, hf)(c))):
                                ins = nc.tensor.matmul(bank[b][:], l, r, start=(c == 0 and t == 0), stop=(c == KD - 1 and t == 2))
                        end(ins, b)
                    pe.wait_ge(e2_hi_done, e + 1)
                    pe.wait_ge(e2_lo_done, e + 1)
                    for t8 in range(TT):
                        hf = t8 // TH
                        if t8 % TH == 0:
                            pe.wait_ge(eg_hi_done, e * NH * KE + (hf + 1) * KE)
                            pe.wait_ge(eg_lo_done, e * NH * KE + (hf + 1) * KE)
                        b, _, need = order.at[("rest", t8 % 4)]
                        pe.wait_ge(drained[b], e * (TT // 4) + need + t8 // 4)
                        ts_ = slice(t8 * P, (t8 + 1) * P)
                        for c in range(KE):
                            for t, (l, r) in enumerate(three((g_hi[:, c, ts_], g_lo[:, c, ts_]), (e2_hi[:, c, :], e2_lo[:, c, :]))):
                                ins = nc.tensor.matmul(bank[b][:, 0:D], l, r, start=(c == 0 and t == 0), stop=(c == KE - 1 and t == 2))
                        end(ins, b)

            slot_tiles = [(k, P) for k in range(ST - 1)] + [(ST - 1, LAST)]

            def turn(s):
                for dt in range(KD):
                    for k, n in slot_tiles:
                        ins = nc.tensor.transpose(bank[4 + dt][:, k * P:k * P + n], xe_tok[s][0:n, k, dt * P:(dt + 1) * P], ident[0:n, 0:n])
                    end(ins, 4 + dt)

            def expert(i, s, last):
                e = i * 2 + s
                pe.wait_ge(w1_hi_done, e + 1)
                pe.wait_ge(w1_lo_done, e + 1)
                pe.wait_ge(xe_hi_done, e * KD + KD)
                pe.wait_ge(xe_lo_done, e * KD + KD)
                for f in range(KE):
                    b, _, need = order.at[("s1", f % 4)]
                    pe.wait_ge(drained[b], e * (KE // 4) + need + f // 4)
                    for c in range(KD):
                        for t, (l, r) in enumerate(three([w[s][:, c, f * P:(f + 1) * P] for w in (w1_hi, w1_lo)], (xe_hi[s][:, c, :], xe_lo[s][:, c, :]))):
                            ins = nc.tensor.matmul(bank[b][:, 0:CAP], l, r, start=(c == 0 and t == 0), stop=(c == KD - 1 and t == 2))
                    end(ins, b)
                if not last:
                    pe.wait_ge(xe_in[1 - s], i * 32 + (32 if s == 0 else 64))
                    turn(1 - s)
                pe.wait_ge(w2_hi_done, e + 1)
                pe.wait_ge(w2_lo_done, e + 1)
                for k, n in slot_tiles:
                    b, _, need = order.at[("rest", 2 + k % 2)]
                    per = 1 if k % 2 else 2
                    pe.wait_ge(drained[b], e * per + need + k // 2)
                    for c in range(KE):
                        if k == 0:
                            pe.wait_ge(own_lo_done, e * KE + c + 1)
                        for t, (l, r) in enumerate(three([g[:, c, k * P:k * P + n] for g in (own_hi, own_lo)], (w2_hi[s][:, c, :], w2_lo[s][:, c, :]))):
                            ins = nc.tensor.matmul(bank[b][0:n, 0:D], l, r, start=(c == 0 and t == 0), stop=(c == KE - 1 and t == 2))
                    end(ins, b)

            ov = overflowed(pe)
            with pe.If(ov == 0):
                for j in range(2):
                    b, _, need = order.at[("rest", j)]
                    pe.wait_ge(drained[b], need)
                pe.wait_ge(xe_in[0], 32)
                turn(0)
                with pe.Fori(0, E // 2 - 1) as i:
                    expert(i, 0, False)
                    expert(i, 1, False)
                expert(E // 2 - 1, 0, False)
                expert(E // 2 - 1, 1, True)
            with pe.Else():
                all_experts()

        @block.scalar
        def _(act):
            def full(key):
                b, n, _ = order.at[key]
                act.wait_ge(filled[b], n)
                return b, bank[b]

            def until_drained(key, times=1):
                b, _, before_ = order.at[key]
                act.wait_ge(drained[b], before_ + times)

            hs = [slice(h * HT, (h + 1) * HT) for h in range(NH)]
            for n, (name, k) in enumerate(names):
                v = I["L0_attn_" + name]
                v = v.rearrange("(k p) -> k p", p=P) if name != "conv_w" else v.rearrange("t (k p) -> (t k) p", p=P)
                act.dma_start(rows[row[name]:row[name] + k, :], v).then_inc(vec_in, 16)
            act.dma_start(rows_e[0:E * KE, :], I["L0_ffn_b1"].rearrange("e (k p) -> (e k) p", p=P)).then_inc(ffn_in, 16)
            act.dma_start(gate_w[:], packed(I["L0_ffn_gate_w"])).then_inc(ffn_in, 16)
            act.dma_start(b2_row[0:E, :], I["L0_ffn_b2"]).then_inc(ffn_in, 16)
            act.wait_ge(c_in, 16)
            nc.scalar.activation(c_row[0:B, :], c_row[0:B, :], ACT.Silu).then_inc(silu_done, 1)

            def a_hi(n):
                act.wait_ge(a_in[n], 16)
                nc.scalar.activation(wa_hi[:, n], raw_a[:, n], ACT.Copy).then_inc(wa_hi_done, 1)

            def m_hi(n):
                act.wait_ge(m_in[n], 16)
                nc.scalar.activation(wm_hi[:, n], raw_m[:, n], ACT.Copy).then_inc(wm_hi_done, 1)

            def ln_root(n):
                hf = (n - 1) % NH
                act.wait_ge(mv_done, n)
                nc.scalar.activation(std[:, hf * TH:(hf + 1) * TH], mv[:, hf * TH:(hf + 1) * TH, 1], ACT.Sqrt,
                                     bias=eps_ln).then_inc(std_done, 1)

            def squares(hf, key, times):
                for dt in range(KD):
                    until_drained((key, hf, dt), times)
                    nc.scalar.activation(square[:, dt, hs[hf]], hT[:, dt, hs[hf]], ACT.Square).then_inc(square_done, 1)

            def mean_root(key, hf):
                b, ps = full(key)
                nc.scalar.activation(rms[:, hf, :], ps[:, 0:TH], ACT.Sqrt, bias=eps_rms, scale=1.0 / D).then_inc(drained[b], 1)

            def hi_of_n(hf, key):
                for dt in range(KD):
                    until_drained(key, dt + 1)
                    nc.scalar.activation(n_hi[:, dt, hs[hf]], xn[:, dt, hs[hf]], ACT.Copy).then_inc(n_hi_done, 1)

            act.wait_ge(consts_done, 2)
            ln_root(1)
            ln_root(2)
            squares(0, "xh", 2)
            mean_root(("ms", 0), 0)
            squares(1, "xh", 2)
            mean_root(("ms", 1), 1)
            a_hi(0)
            hi_of_n(0, ("rb", 0))
            a_hi(1)
            until_drained("vec")
            act.wait_ge(lru_done, 1)

            def right(hf, m):
                n = hf * KH + m
                b, ps = full(("right", hf, m))
                nc.scalar.activation(rbuf[:, n, :, PAD:], ps[:].rearrange("p (b s) -> p b s", b=BH), ACT.Identity,
                                     bias=C("right_b", m)).then_inc(drained[b], 1)
                nc.scalar.activation(u[:, m, hs[hf]], ps[:], ACT.Identity, bias=lru[:, 7, m:m + 1],
                                     scale=C("conv_w", PAD * KH + m)).then_inc(drained[b], 1)

            def u_hi_of(n):
                hf, m = n // KH, n % KH
                act.wait_ge(conv_done, n + 1)
                nc.scalar.activation(u_hi[:, m, hs[hf]], u[:, m, hs[hf]], ACT.Copy).then_inc(u_hi_done, 1)
            right(0, 0)
            right(0, 1)
            hi_of_n(1, ("rb", 1))
            a_hi(2)
            u_hi_of(0)
            right(1, 0)
            u_hi_of(1)
            right(1, 1)
            a_hi(3)
            act.wait_ge(abs_done, 1)
            nc.scalar.activation(lru[:, 1, :], lru[:, 1, :], ACT.Exp).then_inc(abs_done, 1)
            u_hi_of(2)
            u_hi_of(3)
            a_hi(4)
            for hf in range(NH):
                for m in range(KH):
                    b, ps = full(("left", hf, m))
                    nc.scalar.activation(gel[:, m, hs[hf]], ps[:], ACT.Gelu, bias=C("left_b", m)).then_inc(drained[b], 1)
            for hf in range(NH):
                for dt in range(KD):
                    b, ps = full(("xr", hf, dt))
                    nc.scalar.activation(xT[:, dt, hs[hf]], ps[:], ACT.Copy).then_inc(drained[b], 1)
            m_hi(2)
            full(("gb", 1))
            for hf in range(NH):
                for m in range(KH):
                    for g, bias in enumerate(("ga_b", "gx_b")):
                        b, ps = full(("gate", hf, m, g))
                        nc.scalar.activation(tmp[:, 4 * g + hf * KH + m, :], ps[:], ACT.Sigmoid, bias=C(bias, m)).then_inc(drained[b], 1)
            act.wait_ge(lru_done, 2)
            for k in range(4):
                m = k % KH
                until_drained(("gate", k // KH, m, 0))
                nc.scalar.activation(tmp[:, 8 + k, :], tmp[:, k, :], ACT.Exp, scale=lru[:, 5, m:m + 1]).then_inc(lru_out, 1)
                act.wait_ge(lru_out, 2 * k + 1)
                nc.scalar.activation(tmp[:, k, :], tmp[:, k, :], ACT.Tanh, scale=lru[:, 6, m:m + 1]).then_inc(lru_out, 1)
            for k in range(4):
                act.wait_ge(lru_out, 2 * k + 2)
                nc.scalar.activation(tmp[:, k, :], tmp[:, k, :], ACT.Sqrt).then_inc(root_out, 1)
            m_hi(0)
            m_hi(1)
            for n in range(NH * KH):
                act.wait_ge(y_done, n + 1)
                nc.scalar.activation(y_hi[:, n % KH, hs[n // KH]], u[:, n % KH, hs[n // KH]], ACT.Copy).then_inc(y_hi_done, 1)
            for hf in range(NH):
                squares(hf, "out", 1)
                mean_root(("ms2", hf), hf)
            for hf in range(NH):
                hi_of_n(hf, ("rb2", hf))

            def v_hi_of(n):
                until_drained(("up2", n // KF, n % KF))
                nc.scalar.activation(v_hi[:, n % KF, hs[n // KF]], tmp[:, 4 + n % 4, :], ACT.Copy).then_inc(v_hi_done, 1)
            for n in range(NH * KF):
                b, ps = full(("up1", n // KF, n % KF))
                if n >= 4:
                    until_drained(("up2", (n - 4) // KF, (n - 4) % KF))
                nc.scalar.activation(tmp[:, n % 4, :], ps[:], ACT.Gelu, bias=C("up1_b", n % KF)).then_inc(drained[b], 1)
                if n >= 1:
                    v_hi_of(n - 1)
            v_hi_of(NH * KF - 1)
            act.wait_ge(raw2_in, 16)
            nc.scalar.activation(w2_hi[0][:], e_raw2[:].rearrange("p (k n) -> p k n", k=KE), ACT.Copy).then_inc(w2_hi_done, 1)
            act.wait_ge(raw1_in, 16)
            nc.scalar.activation(w1_hi[0][:], e_raw1[:].rearrange("p (k n) -> p k n", k=KD), ACT.Copy).then_inc(w1_hi_done, 1)
            ln_root(3)
            ln_root(4)
            for hf in range(NH):
                for p in range(2):
                    until_drained(("x2t", hf, p))
                    b, ps = full(("x2t", hf, p))
                    nc.scalar.activation(x2_tok[:, hf * TH + 2 * p:hf * TH + 2 * p + 2, :], ps[:].rearrange("p (q d) -> p q d", q=2),
                                         ACT.Copy).then_inc(drained[b], 1)
            until_drained("logits", 2)
            nc.scalar.activation(rt[:, 1, :, :], rt[:, 0, :, :], ACT.Exp).then_inc(exp_done, 1)
            for p in range(TT // 2):
                b, ps = full(("h2t", p))
                nc.scalar.activation(h2_tok[:, 2 * p:2 * p + 2, :], ps[:].rearrange("p (q d) -> p q d", q=2), ACT.Copy).then_inc(drained[b], 1)

            def all_experts():
                act.wait_ge(w2_lo_done, 1)
                for hf in range(NH):
                    for dt in range(KD):
                        nc.scalar.activation(n_hi[:, dt, hs[hf]], hT[:, dt, hs[hf]], ACT.Copy).then_inc(h2_hi, 1)
                act.wait_ge(rest_done, TT // 2)
                with act.Fori(0, E) as e:
                    act.wait_ge(raw1_in, e * 16 + 32)
                    nc.scalar.activation(e1_hi[:], e_raw1[:].rearrange("p (k n) -> p k n", k=KD), ACT.Copy).then_inc(e1_hi_done, 1)
                    nc.scalar.activation(b1_now[:], b1c[:, bass.ds(e * KE, KE)], ACT.Copy).then_inc(bias_done, 1)
                    act.wait_ge(bias_done, e + 1)
                    for n in range(NH * KE):
                        hf, f = n // KE, n % KE
                        b, base, before_ = order.at[("s1", n % 4)]
                        act.wait_ge(filled[b], e * (NH * KE // 4) + base + n // 4 + 1)
                        act.wait_ge(g_free, e * NH * KE + n + 1)
                        nc.scalar.activation(g_raw[:, n % 4, :], bank[b][:], ACT.Gelu,
                                             bias=b1_now[:, f:f + 1]).then_inc(drained[b], 1)
                        act.wait_ge(drained[b], e * (NH * KE // 4) + before_ + n // 4 + 1)
                        nc.scalar.activation(g_hi[:, f, hs[hf]], g_raw[:, n % 4, :], ACT.Copy).then_inc(eg_hi_done, 1)
                        if n == 3:
                            act.wait_ge(raw2_in, e * 16 + 32)
                            nc.scalar.activation(e2_hi[:], e_raw2[:].rearrange("p (k n) -> p k n", k=KE), ACT.Copy).then_inc(e2_hi_done, 1)

            def x_hi(e, s):
                for dt in range(KD):
                    b, base, _ = order.at[("rest", dt)]
                    act.wait_ge(filled[b], e + base + 1)
                    nc.scalar.activation(xe_hi[s][:, dt, :], bank[b][:, 0:CAP], ACT.Copy).then_inc(xe_hi_done, 1)

            def expert(i, s, last):
                e = i * 2 + s
                act.wait_ge(bias_done, e + 1)
                for f in range(KE):
                    b, base, _ = order.at[("s1", f % 4)]
                    act.wait_ge(filled[b], e * (KE // 4) + base + f // 4 + 1)
                    if f >= 4:
                        act.wait_ge(own_lo_done, e * KE + f - 3)
                    nc.scalar.activation(own_raw[:, f % 4, :], bank[b][:, 0:CAP], ACT.Gelu, bias=b1_own[:, s, f:f + 1]).then_inc(drained[b], 1)
                    if f == 1 and not last:
                        act.wait_ge(raw1_in, e * 16 + 32)
                        nc.scalar.activation(w1_hi[1 - s][:], e_raw1[:].rearrange("p (k n) -> p k n", k=KD), ACT.Copy).then_inc(w1_hi_done, 1)
                if not last:
                    x_hi(e + 1, 1 - s)
                    act.wait_ge(raw2_in, e * 16 + 32)
                    nc.scalar.activation(w2_hi[1 - s][:], e_raw2[:].rearrange("p (k n) -> p k n", k=KE), ACT.Copy).then_inc(w2_hi_done, 1)

            ov = overflowed(act)
            with act.If(ov == 0):
                x_hi(0, 0)
                with act.Fori(0, E // 2 - 1) as i:
                    expert(i, 0, False)
                    expert(i, 1, False)
                expert(E // 2 - 1, 0, False)
                expert(E // 2 - 1, 1, True)
            with act.Else():
                all_experts()

        @block.vector
        def _(dve):
            st = Steps(dve, dve_step)

            def full(key):
                b, n, _ = order.at[key]
                dve.wait_ge(filled[b], n)
                return b, bank[b]

            def until_drained(key, times=1):
                b, _, before_ = order.at[key]
                dve.wait_ge(drained[b], before_ + times)

            hs = [slice(h * HT, (h + 1) * HT) for h in range(NH)]
            nc.vector.memset(small[:, 0:1], 1.0).then_inc(consts_done, 1)
            nc.vector.memset(small[:, 1:2], 1e-5)
            nc.vector.memset(small[:, 2:3], 1e-8).then_inc(consts_done, 1)
            pads = st.mark(nc.vector.memset(rbuf[:, :, :, 0:PAD], 0.0))
            for e in range(E):
                slot_base_ready = st.mark(nc.vector.memset(slot_base[:, e:e + 1], float(e * CAP + 1)))
            dve.sem_inc(g_free, 4)
            for s in range(2):
                dve.sem_inc(y_out[s], 32)

            def ln_stats(tile):
                for j, src in tile:
                    last = nc.vector.bn_stats(stat[:, j, :], src)
                st.link(last)
                for j, _ in tile:
                    last = nc.vector.bn_aggr(mv[:, j, :], stat[:, j, :])
                last.then_inc(mv_done, 1)

            def ln_apply(tile, dst, n, empties=None):
                hf = (n - 1) % NH
                dve.wait_ge(std_done, n)
                st.link(nc.vector.reciprocal(rstd[:, hf * TH:(hf + 1) * TH], std[:, hf * TH:(hf + 1) * TH]))
                for k, (j, src) in enumerate(tile):
                    last = nc.vector.tensor_scalar(dst[:, j, :], src, mv[:, j, 0:1], rstd[:, j:j + 1], ALU.subtract, ALU.mult)
                    if empties and k % 2 == 1:
                        last.then_inc(drained[empties[k // 2]], 1)
                return last

            def x_tiles(hf):
                return [(j, x_tok[:, j, :]) for j in range(hf * TH, (hf + 1) * TH)]

            dve.wait_ge(x_in[0], 16)
            ln_stats(x_tiles(0))
            b, ps = full("cT")
            nc.vector.tensor_copy(cT[:], ps[:, 0:KD * B].rearrange("p (k b) -> p k b", k=KD)).then_inc(drained[b], 1)
            ln_apply(x_tiles(0), xhat, 1).then_inc(xhat_done, 1)
            dve.wait_ge(x_in[1], 16)
            ln_stats(x_tiles(1))
            b, ps = full("vec")
            nc.vector.tensor_copy(cols[:], ps[:, 0:NV]).then_inc(drained[b], 1)
            b, ps = full("mod")
            nc.vector.tensor_copy(mod[:], ps[:, 0:12 * B].rearrange("p (j b) -> p j b", b=B)).then_inc(drained[b], 1)
            until_drained("mod")
            st.mark(nc.vector.tensor_scalar(mod[:, 2 * CA:2 * CA + 2, :], mod[:, 2 * CA:2 * CA + 2, :], 1.0, None, ALU.add))
            scales = st.mark(nc.vector.tensor_scalar(mod[:, 2 * CB:2 * CB + 2, :], mod[:, 2 * CB:2 * CB + 2, :], 1.0, None, ALU.add))
            ln_apply(x_tiles(1), xhat, 2).then_inc(xhat_done, 1)
            st.need(scales)

            def modulate(key, hf, scale, shift):
                for dt in range(KD):
                    b, ps = full((key, hf, dt))
                    for q in range(BH):
                        bb = hf * BH + q
                        nc.vector.tensor_scalar(hT[:, dt, bb * S:(bb + 1) * S], ps[:, q * S:(q + 1) * S],
                                                M(scale, dt, bb), M(shift, dt, bb), ALU.mult, ALU.add).then_inc(drained[b], 1)

            modulate("xh", 0, CA, SA)
            modulate("xh", 1, CA, SA)

            def rms_inverse(key, hf, n):
                until_drained(key)
                nc.vector.reciprocal(rinv[:, hf, :], rms[:, hf, :]).then_inc(rinv_done, 1)

            def rms_apply(key, hf, src, w):
                b, ps = full(key)
                for dt in range(KD):
                    until_drained((src[0], hf, dt), src[1])
                for dt in range(KD):
                    ins = nc.vector.scalar_tensor_tensor(out=xn[:, dt, hs[hf]], in0=hT[:, dt, hs[hf]], scalar=C(w, dt), in1=ps[:],
                                                         op0=ALU.mult, op1=ALU.mult)
                    ins.then_inc(drained[b], 1)
                until_drained(key, 2)

            def rms_lo(key, hf, n):
                b, _, _ = order.at[key]
                for dt in range(KD):
                    dve.wait_ge(n_hi_done, KD * (n - 1) + dt + 1)
                    ins = nc.vector.tensor_tensor(n_lo[:, dt, hs[hf]], xn[:, dt, hs[hf]], n_hi[:, dt, hs[hf]].bitcast(F32), ALU.subtract)
                    ins.then_inc(n_lo_done, 1)

            until_drained("vec")
            st.link(nc.vector.tensor_tensor(lru[:, 0, :], cols[:, row["right_b"]:row["right_b"] + KH],
                                            cols[:, row["conv_w"] + PAD * KH:row["conv_w"] + TAPS * KH], ALU.mult))
            nc.vector.tensor_tensor(lru[:, 7, :], lru[:, 0, :], cols[:, row["conv_b"]:row["conv_b"] + KH], ALU.add).then_inc(lru_done, 1)
            rms_inverse(("ms", 0), 0, 1)
            rms_inverse(("ms", 1), 1, 2)
            rms_apply(("rb", 0), 0, ("xh", 2), "norm1_w")
            rms_lo(("rb", 0), 0, 1)
            b, ps = full("b1")
            nc.vector.tensor_copy(b1c[:], ps[:, 0:E * KE]).then_inc(drained[b], 1)

            def bounded(g, s1, s2):
                st.mark(nc.vector.tensor_scalar(s1, g, 0.0, 2.0, ALU.is_ge, ALU.mult))
                st.link(nc.vector.tensor_scalar(s2, g, -1.0, None, ALU.mult))
                st.link(nc.vector.tensor_tensor(s2, s2, g, ALU.max))
                st.link(nc.vector.tensor_scalar(s2, s2, 0.25, None, ALU.max))
                st.link(nc.vector.scalar_tensor_tensor(out=g, in0=s1, scalar=-1.0, in1=s2, op0=ALU.add, op1=ALU.mult))
            for g in range(2):
                b, ps = full(("gb", g))
                nc.vector.tensor_copy(gbb[:, 2 * g:2 * g + 2, :], ps[:].rearrange("p (b d) -> p b d", b=2)).then_inc(drained[b], 1)
            until_drained(("gb", 0))
            until_drained(("gb", 1))
            for g in range(B):
                bounded(gbb[:, g, :], tmp[:, 6, 0:D], tmp[:, 7, 0:D])
            for which in (GA, GB):
                bounded(mod[:, 2 * which:2 * which + 2, :], small[:, 8:16].rearrange("p (k b) -> p k b", k=2),
                        small[:, 16:24].rearrange("p (k b) -> p k b", k=2))

            def conv(n):
                hf, m = n // KH, n % KH
                until_drained(("right", hf, m), 2)
                for k in range(PAD):
                    ins = nc.vector.scalar_tensor_tensor(
                        out=u[:, m, hs[hf]].rearrange("p (b s) -> p b s", b=BH), in0=rbuf[:, n, :, k:k + S],
                        scalar=C("conv_w", k * KH + m), in1=u[:, m, hs[hf]].rearrange("p (b s) -> p b s", b=BH),
                        op0=ALU.mult, op1=ALU.add)
                    if k < PAD - 1:
                        st.link(ins)
                ins.then_inc(conv_done, 1)

            st.need(pads)
            for n in range(NH * KH):
                conv(n)
                if n == 1:
                    rms_apply(("rb", 1), 1, ("xh", 2), "norm1_w")
                    rms_lo(("rb", 1), 1, 2)
            a_par = cols[:, row["a_param"]:row["a_param"] + KH]
            st.link(nc.vector.tensor_scalar(lru[:, 0, :], a_par, -1.0, None, ALU.mult))
            nc.vector.tensor_tensor(lru[:, 1, :], lru[:, 0, :], a_par, ALU.min).then_inc(abs_done, 1)
            dve.wait_ge(abs_done, 2)
            st.link(nc.vector.tensor_scalar(lru[:, 2, :], lru[:, 1, :], 2.0, None, ALU.add))
            st.link(nc.vector.reciprocal(lru[:, 2, :], lru[:, 2, :]))
            st.link(nc.vector.tensor_tensor(lru[:, 2, :], lru[:, 2, :], lru[:, 1, :], ALU.mult))
            st.link(nc.vector.tensor_tensor(lru[:, 3, :], lru[:, 2, :], lru[:, 2, :], ALU.mult))
            SERIES = 9
            st.link(nc.vector.tensor_scalar(lru[:, 4, :], lru[:, 3, :], 1.0 / (2 * SERIES + 1), None, ALU.mult))
            for k in range(SERIES - 1, 0, -1):
                st.link(nc.vector.scalar_tensor_tensor(out=lru[:, 4, :], in0=lru[:, 4, :], scalar=1.0 / (2 * k + 1), in1=lru[:, 3, :],
                                                       op0=ALU.add, op1=ALU.mult))
            st.link(nc.vector.scalar_tensor_tensor(out=lru[:, 4, :], in0=lru[:, 4, :], scalar=1.0, in1=lru[:, 2, :], op0=ALU.add, op1=ALU.mult))
            st.link(nc.vector.tensor_scalar(lru[:, 3, :], a_par, 0.0, 0.5, ALU.max, ALU.mult))
            st.link(nc.vector.tensor_tensor(lru[:, 3, :], lru[:, 3, :], lru[:, 4, :], ALU.add))
            st.link(nc.vector.tensor_scalar(lru[:, 5, :], lru[:, 3, :], -16.0, None, ALU.mult))
            nc.vector.tensor_scalar(lru[:, 6, :], lru[:, 3, :], 8.0, None, ALU.mult).then_inc(lru_done, 1)

            dve.wait_ge(u_lo_done, NH * KH)

            def u_of(k):
                return u[:, k % KH, hs[k // KH]]
            for k in range(4):
                until_drained(("gate", k // KH, k % KH, 1))
                iu = st.mark(nc.vector.tensor_tensor(u_of(k), u_of(k), tmp[:, 4 + k, :], ALU.mult))
            st.need(iu)
            for k in range(4):
                dve.wait_ge(root_out, k + 1)
                st.link(nc.vector.scalar_tensor_tensor(out=tmp[:, k, :], in0=tmp[:, 8 + k, :], scalar=1.0, in1=tmp[:, k, :],
                                                       op0=ALU.add, op1=ALU.mult))
                st.link(nc.vector.tensor_tensor(u_of(k), u_of(k), tmp[:, k, :], ALU.mult))
                for q in range(BH):
                    uq = u_of(k)[:, q * S:(q + 1) * S]
                    last = st.mark(nc.vector.tensor_tensor_scan(uq, tmp[:, 8 + k, q * S:(q + 1) * S], uq, 0.0, ALU.mult, ALU.add))
                st.need(last)
                until_drained(("left", k // KH, k % KH))
                nc.vector.tensor_tensor(u_of(k), gel[:, k % KH, hs[k // KH]], u_of(k), ALU.mult).then_inc(y_done, 1)
            for hf in range(NH):
                for dt in range(KD):
                    b, ps = full(("out", hf, dt))
                    nc.vector.scalar_tensor_tensor(out=hT[:, dt, hs[hf]], in0=ps[:], scalar=C("out_b", dt), in1=hT[:, dt, hs[hf]],
                                                   op0=ALU.add, op1=ALU.add).then_inc(drained[b], 1)
            for hf in range(NH):
                rms_inverse(("ms2", hf), hf, hf + 3)
            for hf in range(NH):
                rms_apply(("rb2", hf), hf, ("out", 1), "norm2_w")
                rms_lo(("rb2", hf), hf, hf + 3)
            for n in range(NH * KF):
                hf, m = n // KF, n % KF
                until_drained(("up1", hf, m))
                b, ps = full(("up2", hf, m))
                if n >= 4:
                    dve.wait_ge(v_lo_done, n - 3)
                nc.vector.scalar_tensor_tensor(out=tmp[:, 4 + n % 4, :], in0=ps[:], scalar=C("up2_b", m), in1=tmp[:, n % 4, :],
                                               op0=ALU.add, op1=ALU.mult).then_inc(drained[b], 1)
            until_drained(("xr", 1, 1))
            for hf in range(NH):
                for dt in range(KD):
                    b, ps = full(("down", hf, dt))
                    nc.vector.scalar_tensor_tensor(out=tmp[:, 8 + dt, :], in0=ps[:], scalar=C("down_b", dt), in1=hT[:, dt, hs[hf]],
                                                   op0=ALU.add, op1=ALU.add).then_inc(drained[b], 1)
                    until_drained(("down", hf, dt))
                    for q in range(BH):
                        bb = hf * BH + q
                        xs = xT[:, dt, bb * S:(bb + 1) * S]
                        ins = nc.vector.scalar_tensor_tensor(out=xs, in0=tmp[:, 8 + dt, q * S:(q + 1) * S], scalar=M(GA, dt, bb), in1=xs,
                                                             op0=ALU.mult, op1=ALU.add)
                        ins.then_inc(x2_done if q else x2_half, 1)

            def x2_tiles(hf):
                out_ = []
                for p in range(2):
                    b, ps = full(("x2t", hf, p))
                    out_ += [(hf * TH + 2 * p + q, ps[:, q * D:(q + 1) * D]) for q in range(2)]
                return out_
            for hf in range(NH):
                tiles = x2_tiles(hf)
                ln_stats(tiles)
                ln_apply(tiles, xhat2, hf + 3, [order.at[("x2t", hf, p)][0] for p in range(2)])
                dve.wait_ge(drained[order.at[("x2t", hf, 1)][0]], order.at[("x2t", hf, 1)][2] + 1)
                dve.sem_inc(xhat_done, 1)
            for hf in range(NH):
                modulate("xh2", hf, CB, SB)
            b, ps = full("logits")
            lg = ps[:, 0:TT * E].rearrange("p (t e) -> p t e", e=E)
            big = small[:, 24:24 + TT]
            nc.vector.tensor_reduce(big, lg, mybir.AxisListType.X, ALU.max).then_inc(drained[b], 1)
            until_drained("logits")
            nc.vector.tensor_tensor(rt[:, 0, :, :], lg, big.rearrange("p (t e) -> p t e", e=1).to_broadcast([P, TT, E]), ALU.subtract).then_inc(drained[b], 1)
            dve.wait_ge(exp_done, 1)
            pe_ = rt[:, 1, :, :]
            mine = pe_.rearrange("p t (e o) -> p t e o", o=1).to_broadcast([P, TT, E, E])
            other = pe_.rearrange("p t (o e) -> p t o e", o=1).to_broadcast([P, TT, E, E])
            beats = tmp[:, 0, :].rearrange("p (t e o) -> p t e o", t=TT, e=E)
            ties = tmp[:, 1, :].rearrange("p (t e o) -> p t e o", t=TT, e=E)
            st.mark(nc.vector.tensor_tensor(beats, other, mine, ALU.is_gt))
            st.link(nc.vector.tensor_tensor(ties, other, mine, ALU.is_equal))
            dve.wait_ge(ident_done, 3)
            st.link(nc.vector.tensor_tensor(ties, ties, before[:].rearrange("p (t e) o -> p t e o", t=1).to_broadcast([P, TT, E, E]), ALU.mult))
            st.link(nc.vector.tensor_tensor(beats, beats, ties, ALU.add))
            rank = rt[:, 2, :, :]
            st.link(nc.vector.tensor_reduce(rank, beats, mybir.AxisListType.X, ALU.add))
            sel = rt[:, 6, :, :]
            nc.vector.tensor_scalar(sel, rank, 2.0, None, ALU.is_lt).then_inc(sel_done, 1)
            dve.wait_ge(sel_done, 1)
            st.link(nc.vector.tensor_tensor(rt[:, 3, :, :], sel, pe_, ALU.mult))
            st.link(nc.vector.tensor_reduce(big, rt[:, 3, :, :], mybir.AxisListType.X, ALU.add))
            st.link(nc.vector.reciprocal(big, big))
            nc.vector.tensor_tensor(rt[:, 5, :, :], rt[:, 3, :, :], big.rearrange("p (t e) -> p t e", e=1).to_broadcast([P, TT, E]), ALU.mult).then_inc(top_done, 1)
            b, ps = full("places")
            most = small[:, 32:33]
            st.link(nc.vector.tensor_reduce(most, ps[:, TT * E:(TT + 1) * E], mybir.AxisListType.X, ALU.max))
            nc.vector.tensor_scalar(overflow[:], most, float(CAP), None, ALU.is_gt).then_inc(overflow_done, 1)
            slot = rt[:, 7, :, :]
            st.need(slot_base_ready)
            nc.vector.tensor_tensor(slot, ps[:, 0:TT * E].rearrange("p (t e) -> p t e", e=E),
                                    slot_base[:].rearrange("p (t e) -> p t e", t=1).to_broadcast([P, TT, E]), ALU.add).then_inc(drained[b], 1)
            until_drained("places")
            st.link(nc.vector.tensor_tensor(slot, slot, sel, ALU.mult))
            high, both = small[:, 40:40 + TT], small[:, 48:48 + TT]
            st.mark(nc.vector.tensor_reduce(high, slot, mybir.AxisListType.X, ALU.max))
            st.link(nc.vector.tensor_reduce(both, slot, mybir.AxisListType.X, ALU.add))
            nc.vector.scalar_tensor_tensor(out=slot_a[:], in0=both, scalar=-1.0, in1=high, op0=ALU.add, op1=ALU.subtract).then_inc(slots_done, 1)
            nc.vector.tensor_scalar(slot_b[:], high, -1.0, None, ALU.add).then_inc(slots_done, 1)
            is_b = rt[:, 8, :, :]
            high_all = high.rearrange("p (t e) -> p t e", e=1).to_broadcast([P, TT, E])
            st.link(nc.vector.tensor_tensor(is_b, slot, high_all, ALU.is_equal))
            st.link(nc.vector.tensor_tensor(is_b, is_b, rt[:, 5, :, :], ALU.mult))
            st.link(nc.vector.tensor_reduce(w_b[:], is_b, mybir.AxisListType.X, ALU.add))
            st.link(nc.vector.tensor_tensor(is_b, slot, high_all, ALU.is_lt))
            st.link(nc.vector.tensor_tensor(is_b, is_b, rt[:, 5, :, :], ALU.mult))
            weights = st.mark(nc.vector.tensor_reduce(w_a[:], is_b, mybir.AxisListType.X, ALU.add))
            for g in range(2):
                b, ps = full(f"cwT{g}")
                nc.vector.tensor_copy(cwT[0:E, hs[g]], ps[0:E, :]).then_inc(drained[b], 1)
            for p in range(TT // 2):
                b, ps = full(("b2", p))
                until_drained(("h2t", p))
                for k in range(2):
                    until_drained(("x2t", k, 1), 2)
                pair = lambda x: x[:, 2 * p:2 * p + 2, :]
                g = gbb[:, 2 * p * P // S:2 * p * P // S + 1, :].to_broadcast([P, 2, D])
                part = xhat2[:, 2 * (p % 2):2 * (p % 2) + 2, :]
                nc.vector.tensor_tensor(part, ps[:].rearrange("p (q d) -> p q d", q=2), pair(h2_tok), ALU.add).then_inc(drained[b], 1)
                until_drained(("b2", p))
                st.link(nc.vector.tensor_tensor(part, part, g, ALU.mult))
                nc.vector.tensor_tensor(pair(x2_tok), pair(x2_tok), part, ALU.add).then_inc(rest_done, 1)
            dve.wait_ge(rest_done, TT // 2)
            st.need(weights)
            at_branch = st.n
            ov = overflowed(dve)
            with dve.If(ov == 0):
                def x_lo(e, s):
                    for dt in range(KD):
                        b, base, _ = order.at[("rest", dt)]
                        dve.wait_ge(xe_hi_done, e * KD + dt + 1)
                        nc.vector.tensor_tensor(xe_lo[s][:, dt, :], bank[b][:, 0:CAP], xe_hi[s][:, dt, :].bitcast(F32), ALU.subtract).then_inc(xe_lo_done, 1)

                def expert(i, s, last):
                    e = i * 2 + s
                    nc.vector.tensor_copy(b1_own[:, s, :], b1c[:, bass.ds(e * KE, KE)]).then_inc(bias_done, 1)
                    for f in range(KE):
                        b, _, before_ = order.at[("s1", f % 4)]
                        dve.wait_ge(drained[b], e * (KE // 4) + before_ + f // 4 + 1)
                        nc.vector.tensor_copy(own_hi[:, f, :], own_raw[:, f % 4, :]).then_inc(own_hi_done, 1)
                        dve.wait_ge(own_hi_done, e * KE + f + 1)
                        nc.vector.tensor_tensor(own_lo[:, f, :], own_raw[:, f % 4, :], own_hi[:, f, :].bitcast(F32), ALU.subtract).then_inc(own_lo_done, 1)
                    if not last:
                        x_lo(e + 1, 1 - s)
                    dve.wait_ge(y_out[s], i * 32 + 32)
                    for k in range(ST):
                        n = P if k < ST - 1 else LAST
                        b, base, _ = order.at[("rest", 2 + k % 2)]
                        dve.wait_ge(filled[b], e * (1 if k % 2 else 2) + base + k // 2 + 1)
                        nc.vector.tensor_copy(y_tok[s][0:n, k, :], bank[b][0:n, 0:D]).then_inc(drained[b], 1)
                    for j, per in ((2, 2), (3, 1)):
                        b, _, before_ = order.at[("rest", j)]
                        dve.wait_ge(drained[b], e * per + before_ + per)
                    dve.sem_inc(y_made, 1)
                x_lo(0, 0)
                with dve.Fori(0, E // 2 - 1) as i:
                    expert(i, 0, False)
                    expert(i, 1, False)
                expert(E // 2 - 1, 0, False)
                expert(E // 2 - 1, 1, True)
                for y, w, gathered in ((y_a, w_a, a_gathered), (y_b, w_b, b_gathered)):
                    for t in range(TT):
                        dve.wait_ge(gathered[t], 16)
                        st.link(nc.vector.scalar_tensor_tensor(out=y[:, t, :], in0=y[:, t, :], scalar=w[:, t:t + 1],
                                                               in1=gbb[:, t * P // S, :], op0=ALU.mult, op1=ALU.mult))
                        if y is y_a:
                            last = st.mark(nc.vector.tensor_tensor(x2_tok[:, t, :], x2_tok[:, t, :], y[:, t, :], ALU.add))
                        else:
                            nc.vector.tensor_tensor(y[:, t, :], x2_tok[:, t, :], y[:, t, :], ALU.add).then_inc(acc_done, 1)
                    st.need(last)
            with dve.Else():
                st.n = at_branch
                nc.vector.memset(acc[:], 0.0).then_inc(acc_turn, 1)
                for hf in range(NH):
                    for dt in range(KD):
                        dve.wait_ge(h2_hi, hf * KD + dt + 1)
                        nc.vector.tensor_tensor(n_lo[:, dt, hs[hf]], hT[:, dt, hs[hf]], n_hi[:, dt, hs[hf]].bitcast(F32), ALU.subtract).then_inc(h2_lo, 1)
                with dve.Fori(0, E) as e:
                    for n in range(NH * KE):
                        hf, f = n // KE, n % KE
                        dve.wait_ge(eg_hi_done, e * NH * KE + n + 1)
                        nc.vector.tensor_tensor(g_lo[:, f, hs[hf]], g_raw[:, n % 4, :], g_hi[:, f, hs[hf]].bitcast(F32), ALU.subtract).then_inc(eg_lo_done, 1)
                        dve.wait_ge(eg_lo_done, e * NH * KE + n + 1)
                        dve.sem_inc(g_free, 1)
                    for t8 in range(TT):
                        b, base, before_ = order.at[("rest", t8 % 4)]
                        dve.wait_ge(filled[b], e * (TT // 4) + base + t8 // 4 + 1)
                        dve.wait_ge(acc_turn, e * TT + 1)
                        nc.vector.scalar_tensor_tensor(out=acc[:, t8, :], in0=bank[b][:, 0:D], scalar=rt[:, 5, t8, bass.ds(e, 1)],
                                                       in1=acc[:, t8, :], op0=ALU.mult, op1=ALU.add).then_inc(drained[b], 1)
                        dve.wait_ge(drained[b], e * (TT // 4) + before_ + t8 // 4 + 1)
                        dve.sem_inc(acc_turn, 1)
                for t in range(TT):
                    st.link(nc.vector.tensor_tensor(acc[:, t, :], acc[:, t, :], gbb[:, t * P // S, :], ALU.mult))
                    nc.vector.tensor_tensor(acc[:, t, :], acc[:, t, :], x2_tok[:, t, :], ALU.add).then_inc(acc_done, 1)

        @block.gpsimd
        def _(pool):
            hs = [slice(h * HT, (h + 1) * HT) for h in range(NH)]
            nc.gpsimd.memset(ident[:], 0.0).then_inc(ident_done, 1)
            pool.wait_ge(ident_done, 1)
            nc.gpsimd.affine_select(out=ident[:], in_=ident[:], compare_op=ALU.not_equal, fill=1.0, base=0,
                                    pattern=[[-1, P]], channel_multiplier=1).then_inc(ident_done, 1)
            nc.gpsimd.memset(all_ones[:], 1.0).then_inc(consts2_done, 1)
            nc.gpsimd.memset(earlier[:], 1.0).then_inc(consts2_done, 1)
            pool.wait_ge(consts2_done, 2)
            nc.gpsimd.affine_select(out=earlier[:], in_=earlier[:], compare_op=ALU.is_gt, fill=0.0, base=0,
                                    pattern=[[1, P]], channel_multiplier=-1).then_inc(consts2_done, 1)
            nc.gpsimd.memset(before[:], 1.0).then_inc(pool_step, 1)
            pool.wait_ge(pool_step, 1)
            nc.gpsimd.affine_select(out=before[:], in_=before[:], compare_op=ALU.is_gt, fill=0.0, base=0,
                                    pattern=[[1, E], [-1, E]], channel_multiplier=0).then_inc(ident_done, 1)

            def until_drained(key, times=1):
                b, _, before_ = order.at[key]
                pool.wait_ge(drained[b], before_ + times)

            def lo(dst, whole, hi, done):
                nc.gpsimd.tensor_tensor(dst, whole, hi.bitcast(F32), ALU.subtract).then_inc(done, 1)

            def a_lo(n):
                pool.wait_ge(wa_hi_done, n + 1)
                lo(wa_lo[:, n], raw_a[:, n], wa_hi[:, n], wa_lo_done)

            def m_lo(n, done):
                pool.wait_ge(wm_hi_done, done)
                lo(wm_lo[:, n], raw_m[:, n], wm_hi[:, n], wm_lo_done)

            a_lo(0)
            a_lo(1)
            for n in range(NH * KH):
                hf, m = n // KH, n % KH
                if n == 2:
                    a_lo(2)
                    a_lo(3)
                pool.wait_ge(u_hi_done, n + 1)
                lo(u_lo[:, m, hs[hf]], u[:, m, hs[hf]], u_hi[:, m, hs[hf]], u_lo_done)
            a_lo(4)
            m_lo(2, 1)
            m_lo(0, 2)
            m_lo(1, 3)
            for n in range(NH * KH):
                hf, m = n // KH, n % KH
                pool.wait_ge(y_hi_done, n + 1)
                lo(y_lo[:, m, hs[hf]], u[:, m, hs[hf]], y_hi[:, m, hs[hf]], y_lo_done)
            for n in range(NH * KF):
                hf, m = n // KF, n % KF
                pool.wait_ge(v_hi_done, n + 1)
                lo(v_lo[:, m, hs[hf]], tmp[:, 4 + n % 4, :], v_hi[:, m, hs[hf]], v_lo_done)
            def w_lo(e, s, which):
                if which == 1:
                    pool.wait_ge(w1_hi_done, e + 1)
                    lo(w1_lo[s][:], e_raw1[:].rearrange("p (k n) -> p k n", k=KD), w1_hi[s][:], w1_lo_done)
                else:
                    pool.wait_ge(w2_hi_done, e + 1)
                    lo(w2_lo[s][:], e_raw2[:].rearrange("p (k n) -> p k n", k=KE), w2_hi[s][:], w2_lo_done)
            w_lo(0, 0, 1)
            w_lo(0, 0, 2)
            ov = overflowed(pool)
            with pool.If(ov == 0):
                def scatter(t, rows_, slots, done):
                    nc.gpsimd.indirect_dma_start(rows_, bass.IndirectOffsetOnAxis(ap=slots[:, t:t + 1], axis=0), h2_tok[:, t, :], None).then_inc(done, 16)

                def gather(t, y, rows_, slots, done):
                    nc.gpsimd.indirect_dma_start(y[:, t, :], None, rows_, bass.IndirectOffsetOnAxis(ap=slots[:, t:t + 1], axis=0)).then_inc(done, 16)
                pool.wait_ge(rows_filled, 16 * fills)
                pool.wait_ge(slots_done, 1)
                for t in range(TT):
                    until_drained(("h2t", t // 2))
                    scatter(t, x_rows[0:(E - 1) * CAP], slot_a, a_scattered)
                pool.wait_ge(slots_done, 2)
                pool.wait_ge(a_scattered, 16 * TT)
                for t in range(TT):
                    scatter(t, x_rows, slot_b, b_scattered)

                def expert(i, s):
                    w_lo(i * 2 + s + 1, 1 - s, 1)
                    w_lo(i * 2 + s + 1, 1 - s, 2)
                with pool.Fori(0, E // 2 - 1) as i:
                    expert(i, 0)
                    expert(i, 1)
                expert(E // 2 - 1, 0)
                pool.wait_ge(y_out[0], 32 * (E // 2 + 1))
                pool.wait_ge(y_out[1], 32 * (E // 2))
                for t in range(TT):
                    gather(t, y_a, y_rows[0:(E - 1) * CAP], slot_a, a_gathered[t])
                pool.wait_ge(y_out[1], 32 * (E // 2 + 1))
                for t in range(TT):
                    gather(t, y_b, y_rows, slot_b, b_gathered[t])
            with pool.Else():
                with pool.Fori(0, E) as e:
                    pool.wait_ge(e1_hi_done, e + 1)
                    lo(e1_lo[:], e_raw1[:].rearrange("p (k n) -> p k n", k=KD), e1_hi[:], e1_lo_done)
                    pool.wait_ge(e2_hi_done, e + 1)
                    lo(e2_lo[:], e_raw2[:].rearrange("p (k n) -> p k n", k=KE), e2_hi[:], e2_lo_done)


_OUT_SHAPE = (4, 256, 256)


def kernel(**inputs):
    import numpy as np
    import concourse.bacc as bacc
    from concourse.bass_utils import run_bass_kernel_spmd

    nc = bacc.Bacc("TRN2", target_bir_lowering=False, num_devices=1)
    arrays, aps = {}, {}
    for name, a in inputs.items():
        a = np.ascontiguousarray(a)
        arrays[f"in_{name}"] = a
        aps[name] = nc.dram_tensor(f"in_{name}", a.shape, mybir.dt.from_np(a.dtype), kind="ExternalInput").ap()
    out = nc.dram_tensor("out_x", _OUT_SHAPE, F32, kind="ExternalOutput").ap()
    adaln_block(nc, aps, out)
    return run_bass_kernel_spmd(nc, [arrays], core_ids=[0]).results[0]["out_x"]
```

```python
from contextlib import ExitStack

import concourse.bass as bass
from concourse import mybir

ALU = mybir.AluOpType
ACT = mybir.ActivationFunctionType
F32 = mybir.dt.float32
F32R = mybir.dt.float32r
I32 = mybir.dt.int32
BF16 = mybir.dt.bfloat16

P = 128
HT = 512
CAP = 320


class Order:

    def __init__(self):
        self.filled, self.drained, self.at, self.next = [0] * 8, [0] * 8, {}, 0

    def take(self, key, drains=1, bank=None):
        b = self.next if bank is None else bank
        self.next = (b + 1) % 8
        self.filled[b] += 1
        self.at[key] = (b, self.filled[b], self.drained[b])
        self.drained[b] += drains

    def loop(self, key, bank):
        self.at[key] = (bank, self.filled[bank], self.drained[bank])


class Steps:

    def __init__(self, engine, sem):
        self.engine, self.sem, self.n = engine, sem, 0

    def mark(self, ins):
        ins.then_inc(self.sem, 1)
        self.n += 1
        return self.n

    def need(self, n):
        self.engine.wait_ge(self.sem, n)

    def link(self, ins):
        self.need(self.mark(ins))


def adaln_block(nc, I, out):
    B, S, D = I["L0_attn_x"].shape
    H = I["L0_attn_left_W"].shape[1]
    F = I["L0_attn_up1_W"].shape[1]
    _, E = I["L0_ffn_gate_w"].shape
    FE = I["L0_ffn_w1"].shape[2]
    T = B * S
    NH = T // HT
    TT = T // P
    TH = HT // P
    BH = HT // S
    KD, KH, KF, KE = D // P, H // P, F // P, FE // P
    TAPS = I["L0_attn_conv_w"].shape[0]
    PAD = TAPS - 1
    assert KD == 2 and KH == KD and KF == 6 and NH == 2 and BH == 2 and E == 8 and KE == 8
    EPACK = KD * FE
    assert KE * D == EPACK

    names = [("norm1_w", KD), ("left_b", KH), ("right_b", KH), ("conv_w", TAPS * KH), ("conv_b", KH),
             ("ga_b", KH), ("gx_b", KH), ("a_param", KH), ("out_b", KD), ("norm2_w", KD),
             ("up1_b", KF), ("up2_b", KF), ("down_b", KD)]
    row, NV = {}, 0
    for n, k in names:
        row[n], NV = NV, NV + k

    order = Order()
    for key in ["cT", "mod_a", ("xh", 0, 0), ("xh", 0, 1), ("ms", 0), "vec", ("rb", 0), ("xh", 1, 0), ("xh", 1, 1)]:
        order.take(key, drains=2 if key[0] in ("xh", "rb") else 1)

    def take_side(side, hf):
        for m in range(KH):
            order.take((side, hf, m), drains=2 if side == "right" else 1)
    order.take(("busy", 0), drains=0)
    take_side("right", 0)
    order.take(("ms", 1))
    order.take(("rb", 1), drains=2)
    take_side("left", 0)
    take_side("right", 1)

    def take_gates(hf):
        for m in range(KH):
            for g in range(2):
                order.take(("gate", hf, m, g))

    def take_out(hf):
        for dt in range(KD):
            order.take(("out", hf, dt))
    take_gates(0)
    take_side("left", 1)
    take_gates(1)
    order.take("mod_b")
    order.take(("busy", 3), drains=0)
    take_out(0)
    order.take(("ms2", 0))
    order.take(("rb2", 0), drains=2)
    for key in [("gb", 0), ("gb", 1), "b1"]:
        order.take(key)

    def take_up(hf, m):
        order.take(("up1", hf, m))
        order.take(("up2", hf, m))

    def take_down(hf):
        for dt in range(KD):
            order.take(("down", hf, dt))

    def take_x2t(hf):
        for p in range(2):
            order.take(("x2t", hf, p), drains=2)

    def take_xh2(hf):
        for dt in range(KD):
            order.take(("xh2", hf, dt), drains=2)

    def take_biases(hf):
        for p in range(2):
            order.take(("b2", hf, p))

    def take_h2t(hf):
        for p in range(2):
            order.take(("h2t", hf, p))
    take_up(0, 0)
    take_up(0, 1)
    take_out(1)
    take_up(0, 2)
    for dt in range(KD):
        order.take(("xr", 0, dt))
    order.take(("ms2", 1))
    take_up(0, 3)
    order.take(("rb2", 1), drains=2)
    take_up(0, 4)
    for dt in range(KD):
        order.take(("xr", 1, dt))
    take_up(0, 5)
    take_up(1, 0)
    take_down(0)
    take_up(1, 1)
    take_up(1, 2)
    take_x2t(0)
    take_up(1, 3)
    take_up(1, 4)
    take_xh2(0)
    take_up(1, 5)
    order.take(("logits", 0), drains=2)
    take_h2t(0)
    order.take(("down", 1, 0))
    order.take(("places", 0))
    order.take(("down", 1, 1))
    order.take(("cwT", 0))
    take_x2t(1)
    take_biases(0)
    order.take(("busy", 1), drains=0)
    take_xh2(1)
    order.take(("logits", 1), drains=2)
    take_h2t(1)
    order.take(("places", 1))
    order.take(("cwT", 1))
    take_biases(1)
    order.take(("busy", 2), drains=0)
    for j in range(4):
        order.loop(("s1", j), j)
        order.loop(("rest", j), 4 + j)

    ctx = ExitStack()
    with ctx:
        sem = lambda n: ctx.enter_context(nc.semaphore(n))
        bank = [ctx.enter_context(nc.psum_tensor(f"bank{b}", [P, HT], F32)) for b in range(8)]
        filled = [sem(f"bank_filled{b}") for b in range(8)]
        drained = [sem(f"bank_drained{b}") for b in range(8)]

        SA, CA, GA, SB, CB, GB = range(6)

        top = [(nc.sbuf_base + 31) // 32 * 32]

        def at(name, off, shape, dt=F32):
            return nc.alloc_sbuf_tensor_at(name, [P, *shape], dt, offset=off)

        def region(size):
            off = top[0]
            top[0] += (size + 31) // 32 * 32
            return off

        def new(name, shape, dt=F32):
            n = 4
            for s in shape:
                n *= s
            return at(name, region(n), shape, dt)

        ident = new("ident", [P])
        rows = new("rows", [P])
        rows_e = new("rows_e", [P])
        cols = new("cols", [NV])
        b1c = new("b1c", [E * KE])
        b1_now = new("b1_now", [KE])
        mod = new("mod", [2 * 5, B])
        gbb = new("gbb", [B, D])
        small = new("small", [64])
        c_row = new("c_row", [D])
        cT = new("cT", [KD, B])
        gate_w = new("gate_w", [KD, E])
        b2_row = new("b2_row", [D])
        stat = new("stat", [TT, 6])
        mv = new("mv", [TT, 2])
        std = new("std", [TT])
        rstd = new("rstd", [TT])
        rms = new("rms", [2, TH])
        rinv = new("rinv", [2, TH])
        before = new("before", [E, E])
        earlier, all_ones = new("earlier", [P], BF16), new("all_ones", [P], BF16)
        sel_16 = new("sel_16", [TT, E], BF16)
        slot_base = new("slot_base", [E])
        overflow = new("overflow", [1], I32)
        unused_slots = new("unused_slots", [E])
        slot_a, slot_b = new("slot_a", [TT], I32), new("slot_b", [TT], I32)
        row_a, row_b = new("row_a", [TT], I32), new("row_b", [TT], I32)
        b1_own = new("b1_own", [2, KE])
        w_a, w_b = new("w_a", [TT]), new("w_b", [TT])
        lru = new("lru", [8, KH])
        rt = new("rt", [9, TT, E])
        o_xT = top[0]
        xT = new("xT", [KD, T])
        hT = new("hT", [KD, T])
        o_n = top[0]
        n_hi = new("n_hi", [KD, T], F32R)
        n_lo = new("n_lo", [KD, T], F32R)
        EB = EPACK * 4
        first = [("right", H), ("left", H), ("ga", H), ("gx", H), ("out", D)]
        NA = len(first) * KD * D
        o_wa = top[0]
        wa_hi, wa_lo = new("wa_hi", [len(first), KD, D], F32R), new("wa_lo", [len(first), KD, D], F32R)
        NM = KD * F
        second = ["up1", "up2", "down"]
        o_wm = top[0]
        wm_hi, wm_lo = new("wm_hi", [3, NM], F32R), new("wm_lo", [3, NM], F32R)
        o_raw = region(3 * NM * 4)
        raw_a = at("raw_a", o_raw, [len(first), KD, D])
        raw_m = at("raw_m", o_raw, [3, NM])
        o_x = region(TT * D * 4)
        x_tok, x2_tok = at("x_tok", o_x, [TT, D]), at("x2_tok", o_x, [TT, D])
        o_r1 = region(2 * KF * T * 4)
        TB = KD * T * 4
        u = at("u", o_r1, [KH, T])
        square = at("square", o_r1, [KD, T])
        xn = at("xn", o_r1 + TB, [KD, T])
        gel = at("gel", o_r1 + TB, [KH, T])
        u_hi, u_lo = at("u_hi", o_r1 + 2 * TB, [KH, T], F32R), at("u_lo", o_r1 + 3 * TB, [KH, T], F32R)
        y_hi, y_lo = at("y_hi", o_r1 + 4 * TB, [KH, T], F32R), at("y_lo", o_r1 + 5 * TB, [KH, T], F32R)
        v_hi, v_lo = at("v_hi", o_r1, [KF, T], F32R), at("v_lo", o_r1 + 3 * TB, [KF, T], F32R)
        HB = HT * 4
        o_t = region(12 * HB)
        tmp = at("tmp", o_t, [12, HT])
        wmod = at("wmod", o_wm + 3 * NM * 4, [KD, GB * D])
        wmod_gb = at("wmod_gb", o_xT, [KD, D])
        bound_tmp = at("bound_tmp", o_t + 10 * HB, [2, D])
        xhat = at("xhat", o_t + 6 * HB, [TT, D])
        o_rbuf = top[0]
        rbuf = new("rbuf", [4, BH, S + PAD])
        e_raw1 = at("e_raw1", o_raw, [EPACK])
        e_raw2 = at("e_raw2", o_raw + EB, [EPACK])
        assert 4 * EB <= 6 * NM * 4 and 2 * EB <= 3 * NM * 4
        e1_hi, e1_lo = at("e1_hi", o_wm, [KD, FE], F32R), at("e1_lo", o_wm + EB, [KD, FE], F32R)
        e2_hi, e2_lo = at("e2_hi", o_wm + 2 * EB, [KE, D], F32R), at("e2_lo", o_wm + 3 * EB, [KE, D], F32R)
        rank_tmp = at("rank_tmp", o_t + 8 * HB, [2 * TH * E * E])
        cwT = at("cwT", o_r1 + 3 * TB, [T])
        xhat2 = at("xhat2", o_t + 10 * HB, [TH, D])
        biases = at("biases", o_r1, [TT, D])
        g_hi = at("g_hi", o_r1, [KE, T], F32R)
        g_lo = at("g_lo", o_r1 + KE * T * 4, [KE, T], F32R)
        g_raw = at("g_raw", o_r1 + 2 * KE * T * 4, [4, HT])
        acc = at("acc", o_rbuf, [TT, D])
        assert 2 * KE * T * 4 + 4 * HB <= 2 * KF * T * 4 + 12 * HB
        w1_hi, w1_lo, w2_hi, w2_lo = [], [], [], []
        for s, o in enumerate((o_wa, o_wm)):
            w1_hi.append(at(f"w1_hi{s}", o, [KD, FE], F32R))
            w1_lo.append(at(f"w1_lo{s}", o + EB, [KD, FE], F32R))
        for s, o in enumerate((o_n, o_wm + 2 * EB)):
            w2_hi.append(at(f"w2_hi{s}", o, [KE, D], F32R))
            w2_lo.append(at(f"w2_lo{s}", o + EB, [KE, D], F32R))
        assert 2 * EB <= 2 * NA * 4 and 4 * EB <= 6 * NM * 4 and 2 * EB <= 2 * TB
        h2_tok = at("h2_tok", o_xT, [2, NH, 2, D])
        y_a, y_b = at("y_a", o_r1 + TB, [TT, D]), at("y_b", o_r1 + 2 * TB, [TT, D])
        CB4 = CAP * 4
        own_hi = at("own_hi", o_r1 + 3 * TB, [KE, CAP], F32R)
        own_lo = at("own_lo", o_r1 + 3 * TB + KE * CB4, [KE, CAP], F32R)
        assert 3 * TB + 2 * KE * CB4 <= 2 * KF * T * 4
        ST = (CAP + P - 1) // P
        LAST = CAP - (ST - 1) * P
        own_raw = at("own_raw", o_t, [4, CAP])
        o_c = o_t + 4 * CB4
        xe_hi = [at(f"xe_hi{s}", o_c + 2 * s * CB4, [KD, CAP], F32R) for s in range(2)]
        xe_lo = [at(f"xe_lo{s}", o_c + (4 + 2 * s) * CB4, [KD, CAP], F32R) for s in range(2)]
        xe_tok = [at(f"xe_tok{s}", o_c + 8 * CB4 + s * ST * D * 4, [ST, D]) for s in range(2)]
        assert 12 * CB4 + 2 * ST * D * 4 <= 12 * HB and 2 * ST * D * 4 <= 4 * BH * (S + PAD) * 4
        y_tok = [at(f"y_tok{s}", o_rbuf + s * ST * D * 4, [ST, D]) for s in range(2)]
        assert top[0] <= nc.sbuf_usable_end, (top[0], nc.sbuf_usable_end)
        ones = small[:, 0:1]
        eps_ln, eps_rms = small[:, 1:2], small[:, 2:3]

        def h2_tile(t):
            return h2_tok[:, t // 2 % 2, t // TH, t % 2, :]

        def C(name, k=0):
            return cols[:, row[name] + k:row[name] + k + 1]

        def M(which, dt, b):
            return mod[:, 2 * which + dt, b:b + 1]

        x_view = I["L0_attn_x"].rearrange("b s d -> (b s) d").rearrange("(t p) d -> p t d", p=P)
        out_view = out.rearrange("b s d -> (b s) d").rearrange("(t p) d -> p t d", p=P)

        def packed(w):
            return w.rearrange("(k p) n -> p k n", p=P)

        x_in = [sem(f"x_in{h}") for h in range(NH)]
        vec_in, c_in, ffn_in = sem("vec_in"), sem("c_in"), sem("ffn_in")
        wmod_in, wmod2_in, wmod3_in, vec2_in = sem("wmod_in"), sem("wmod2_in"), sem("wmod3_in"), sem("vec2_in")
        a_in = [sem(f"a_in_{n}") for n, _ in first]
        m_in = [sem(f"m_in_{n}") for n in second]
        wa_hi_done, wa_lo_done, wm_hi_done, wm_lo_done = (sem(n) for n in ("wa_hi_done", "wa_lo_done", "wm_hi_done", "wm_lo_done"))
        ident_done, consts_done = sem("ident_done"), sem("consts_done")
        silu_done = sem("silu_done")
        lru_done = sem("lru_done")
        mv_done, std_done, xhat_done = sem("mv_done"), sem("std_done"), sem("xhat_done")
        square_done, rinv_done = sem("square_done"), sem("rinv_done")
        n_hi_done, n_lo_done = sem("n_hi_done"), sem("n_lo_done")
        conv_done, u_hi_done, u_lo_done = sem("conv_done"), sem("u_hi_done"), sem("u_lo_done")
        lru_out, root_out = sem("lru_out"), sem("root_out")
        y_done, y_hi_done, y_lo_done = sem("y_done"), sem("y_hi_done"), sem("y_lo_done")
        v_hi_done, v_lo_done = sem("v_hi_done"), sem("v_lo_done")
        x2_done = sem("x2_done")
        h2_hi, h2_lo = sem("h2_hi"), sem("h2_lo")
        top_done, exp_done = sem("top_done"), sem("exp_done")
        consts2_done, sel_done = sem("consts2_done"), sem("sel_done")
        overflow_done, slots_done = sem("overflow_done"), sem("slots_done")
        rest_done, rows_done = sem("rest_done"), sem("rows_done")
        rows_filled = sem("rows_filled")
        a_scattered, b_scattered = [sem(f"a_scattered{h}") for h in range(NH)], [sem(f"b_scattered{h}") for h in range(NH)]
        xe_in = [sem(f"xe_in{s}") for s in range(2)]
        xe_hi_done, xe_lo_done = sem("xe_hi_done"), sem("xe_lo_done")
        own_hi_done, own_lo_done = sem("own_hi_done"), sem("own_lo_done")
        y_made = sem("y_made")
        y_out = [sem(f"y_out{s}") for s in range(2)]
        a_gathered = [sem(f"a_gathered{t}") for t in range(TT)]
        b_gathered = [sem(f"b_gathered{t}") for t in range(TT)]
        w1_hi_done, w1_lo_done, w2_hi_done, w2_lo_done = sem("w1_hi_done"), sem("w1_lo_done"), sem("w2_hi_done"), sem("w2_lo_done")
        raw1_in, raw2_in = sem("raw1_in"), sem("raw2_in")
        e1_hi_done, e1_lo_done = sem("e1_hi_done"), sem("e1_lo_done")
        e2_hi_done, e2_lo_done = sem("e2_hi_done"), sem("e2_lo_done")
        eg_hi_done, eg_lo_done = sem("eg_hi_done"), sem("eg_lo_done")
        stored = sem("stored")
        dve_step, pool_step = sem("dve_step"), sem("pool_step")
        acc_done = sem("acc_done")
        g_free, acc_turn = sem("g_free"), sem("acc_turn")
        bias_done = sem("bias_done")
        abs_done, x2_half = sem("abs_done"), sem("x2_half")

        def three(m, n):
            return ((m[0], n[0]), (m[0], n[1]), (m[1], n[0]))

        x_rows = nc.dram_tensor("x_rows", (E * T, D), F32, kind="Internal").ap()
        y_rows = nc.dram_tensor("y_rows", (E * CAP, D), F32, kind="Internal").ap()
        whole = (ST - 1) * P

        def overflowed(engine):
            engine.wait_ge(overflow_done, 1)
            return engine.value_load(overflow[0:1, 0:1], min_val=0, max_val=1)

        def load_vectors(engine, some, done):
            for name, k in some:
                v = I["L0_attn_" + name]
                v = v.rearrange("(k p) -> k p", p=P) if name != "conv_w" else v.rearrange("t (k p) -> (t k) p", p=P)
                engine.dma_start(rows[row[name]:row[name] + k, :], v).then_inc(done, 16)

        block = ctx.enter_context(nc.Block())

        @block.sync
        def _(sp):
            for hf in range(NH):
                sp.dma_start(x_tok[:, hf * TH:(hf + 1) * TH, :], x_view[:, hf * TH:(hf + 1) * TH, :]).then_inc(x_in[hf], 16)
            def load_a(n):
                sp.dma_start(raw_a[:, n], packed(I["L0_attn_" + first[n][0] + "_W"])).then_inc(a_in[n], 16)

            def load_m(n):
                sp.dma_start(raw_m[:, n].rearrange("p (k n) -> p k n", k=KF if second[n] == "down" else KD),
                             packed(I["L0_attn_" + second[n] + "_W"])).then_inc(m_in[n], 16)
            for n in range(4):
                load_a(n)
            sp.dma_start(wmod[:, :, 2 * D:], packed(I["L0_wmod"])[:, :, 2 * D:GB * D]).then_inc(wmod2_in, 16)
            sp.dma_start(wmod_gb[:], packed(I["L0_wmod"])[:, :, GB * D:]).then_inc(wmod3_in, 16)
            load_a(4)
            load_m(2)
            sp.wait_ge(wa_hi_done, len(first))
            sp.wait_ge(wa_lo_done, len(first))
            load_m(0)
            load_m(1)
            sp.wait_ge(wm_hi_done, 3)
            sp.wait_ge(wm_lo_done, 3)
            w1v = I["L0_ffn_w1"].rearrange("e (k p) n -> p e k n", p=P)
            w2v = I["L0_ffn_w2"].rearrange("e (k p) n -> p e k n", p=P)

            def load_w1(e):
                sp.dma_start(e_raw1[:].rearrange("p (e k n) -> p e k n", e=1, k=KD), w1v[:, bass.ds(e, 1)]).then_inc(raw1_in, 16)

            def load_w2(e):
                sp.dma_start(e_raw2[:].rearrange("p (e k n) -> p e k n", e=1, k=KE), w2v[:, bass.ds(e, 1)]).then_inc(raw2_in, 16)
            load_w1(0)
            load_w2(0)
            xr = I["L0_attn_x"].rearrange("b s d -> (b s) d")
            sp.dma_start(x_rows.rearrange("(e c) d -> e c d", c=T)[:, 0:CAP],
                         xr[0:CAP].rearrange("(e c) d -> e c d", e=1).to_broadcast([E, CAP, D])).then_inc(rows_filled, 16)
            sp.wait_ge(rows_filled, 16)
            sp.wait_ge(w1_lo_done, 1)
            load_w1(1)
            sp.wait_ge(w2_lo_done, 1)
            load_w2(1)
            ov = overflowed(sp)
            with sp.If(ov == 0):
                def rows_of(buf, e, room):
                    r = buf.rearrange("(e c) d -> e c d", c=room)[bass.ds(e, 1)]
                    return (r[:, 0:whole].rearrange("e (k p) d -> p (e k) d", p=P), r[:, whole:CAP].rearrange("e c d -> c e d"))

                def load_x(e, s):
                    a, b = rows_of(x_rows, e, T)
                    sp.dma_start(xe_tok[s][:, 0:ST - 1, :], a).then_inc(xe_in[s], 16)
                    sp.dma_start(xe_tok[s][0:LAST, ST - 1:ST, :], b).then_inc(xe_in[s], 16)

                def expert(i, s, to_come):
                    kept = (lambda v: v) if isinstance(i, int) else sp.snap
                    _, f5, _ = order.at[("rest", 1)]
                    e = kept(i * 2 + s)
                    ahead, turned, ahead2 = kept(i * 2 + s + 1), kept(i * 2 + (s + f5)), kept(i * 2 + s + 2)
                    if to_come >= 1:
                        if s == 0:
                            for hf in range(NH):
                                sp.wait_ge(b_scattered[hf], 16 * TH)
                        sp.wait_ge(filled[5], turned)
                        load_x(ahead, 1 - s)
                    if to_come >= 2:
                        sp.wait_ge(w1_lo_done, ahead2)
                        load_w1(ahead2)
                        sp.wait_ge(w2_lo_done, ahead2)
                        load_w2(ahead2)
                    a, b = rows_of(y_rows, e, CAP)
                    sp.wait_ge(y_made, ahead)
                    sp.dma_start(a, y_tok[s][:, 0:ST - 1, :]).then_inc(y_out[s], 16)
                    sp.dma_start(b, y_tok[s][0:LAST, ST - 1:ST, :]).then_inc(y_out[s], 16)
                for hf in range(NH):
                    sp.wait_ge(a_scattered[hf], 16 * TH)
                load_x(0, 0)
                with sp.Fori(0, E // 2 - 1) as i:
                    expert(i, 0, 2)
                    expert(i, 1, 2)
                expert(E // 2 - 1, 0, 1)
                expert(E // 2 - 1, 1, 0)
                for p in range(TT // 2):
                    sp.wait_ge(acc_done, 2 * (p + 1))
                    sp.dma_start(out_view[:, 2 * p:2 * p + 2, :], y_b[:, 2 * p:2 * p + 2, :]).then_inc(stored, 16)
                sp.wait_ge(stored, 16 * (TT // 2))
            with sp.Else():
                for hf in range(NH):
                    sp.wait_ge(a_scattered[hf], 16 * TH)
                    sp.wait_ge(b_scattered[hf], 16 * TH)
                sp.wait_ge(raw1_in, 32)
                sp.wait_ge(raw2_in, 32)
                load_w1(0)
                load_w2(0)
                with sp.Fori(1, E) as e:
                    sp.wait_ge(e1_hi_done, e)
                    sp.wait_ge(e1_lo_done, e)
                    load_w1(e)
                    sp.wait_ge(e2_hi_done, e)
                    sp.wait_ge(e2_lo_done, e)
                    load_w2(e)
                for hf in range(NH):
                    sp.wait_ge(acc_done, (hf + 1) * TH)
                    sp.dma_start(out_view[:, hf * TH:(hf + 1) * TH, :], acc[:, hf * TH:(hf + 1) * TH, :]).then_inc(stored, 16)
                sp.wait_ge(stored, 16 * NH)

        @block.tensor
        def _(pe):
            def begin(key):
                b, _, need = order.at[key]
                if need:
                    pe.wait_ge(drained[b], need)
                return b, bank[b]

            def end(ins, b):
                ins.then_inc(filled[b], 1)

            def until_drained(key, times=1):
                b, _, before_ = order.at[key]
                pe.wait_ge(drained[b], before_ + times)

            def transposes(key, src, n, rows_, step=P):
                b, ps = begin(key)
                for j in range(n):
                    ins = nc.tensor.transpose(ps[:, j * step:j * step + rows_], src(j), ident[0:rows_, 0:rows_])
                end(ins, b)

            def product(key, w, x, k, n=HT):
                b, ps = begin(key)
                for c in range(k):
                    for t, (l, r) in enumerate(three(w(c), x(c))):
                        ins = nc.tensor.matmul(ps[:, 0:n], l, r, start=(c == 0 and t == 0), stop=(c == k - 1 and t == 2))
                end(ins, b)
                return ins

            def mean_square(key, hf, n):
                b, ps = begin(key)
                for dt in range(KD):
                    pe.wait_ge(square_done, KD * n + dt + 1)
                    for j in range(TH):
                        ins = nc.tensor.matmul(ps[:, j:j + 1], square[:, dt, hf * HT + j * P:hf * HT + (j + 1) * P], ones,
                                               start=(dt == 0 and j == 0), stop=(dt == KD - 1 and j == TH - 1))
                end(ins, b)

            def spread(key, hf):
                b, ps = begin(key)
                for j in range(TH):
                    ins = nc.tensor.matmul(ps[:, j * P:(j + 1) * P], rinv[:, hf, j:j + 1].to_broadcast([P, P]), ident[:],
                                           start=True, stop=True)
                end(ins, b)

            hs = [slice(h * HT, (h + 1) * HT) for h in range(NH)]
            pe.wait_ge(ident_done, 2)
            pe.wait_ge(silu_done, 1)
            transposes("cT", lambda j: c_row[0:B, j * P:(j + 1) * P], KD, B, step=B)
            until_drained("cT")

            def modulation(key, js):
                b, ps = begin(key)
                for j in js:
                    for k in range(KD):
                        ins = nc.tensor.matmul(ps[:, j * B:(j + 1) * B], wmod[:, k, j * P:(j + 1) * P], cT[:, k, :],
                                               start=(k == 0), stop=(k == KD - 1))
                end(ins, b)
            pe.wait_ge(wmod_in, 16)
            modulation("mod_a", range(2 * KD))

            def x_blocks(key, hf, src):
                for dt in range(KD):
                    transposes((key, hf, dt), lambda j: src[:, hf * TH + j, dt * P:(dt + 1) * P], TH, P)
            pe.wait_ge(xhat_done, 1)
            x_blocks("xh", 0, xhat)
            pe.wait_ge(consts_done, 2)
            mean_square(("ms", 0), 0, 0)
            pe.wait_ge(vec_in, 16 * len(names[0::2]))
            pe.wait_ge(vec2_in, 16 * len(names[1::2]))
            transposes("vec", lambda j: rows[0:NV, :], 1, NV)
            pe.wait_ge(rinv_done, 1)
            spread(("rb", 0), 0)
            pe.wait_ge(xhat_done, 2)
            x_blocks("xh", 1, xhat)

            def wa(n):
                return lambda m: lambda c: (wa_hi[:, n, c, m * P:(m + 1) * P], wa_lo[:, n, c, m * P:(m + 1) * P])

            def wm(n, k):
                w = [x[:, n].rearrange("p (k n) -> p k n", k=k) for x in (wm_hi, wm_lo)]
                return lambda m: lambda c: tuple(x[:, c, m * P:(m + 1) * P] for x in w)

            def split_of(hi, lo, hf):
                return lambda c: (hi[:, c, hs[hf]], lo[:, c, hs[hf]])

            def wa_ready(n):
                pe.wait_ge(wa_hi_done, n + 1)
                pe.wait_ge(wa_lo_done, n + 1)

            def wm_ready(n):
                pe.wait_ge(wm_hi_done, n)
                pe.wait_ge(wm_lo_done, n)

            def side(name, n, hf):
                pe.wait_ge(n_hi_done, KD * (hf + 1))
                pe.wait_ge(n_lo_done, KD * (hf + 1))
                wa_ready(n)
                for m in range(KH):
                    product((name, hf, m), wa(n)(m), split_of(n_hi, n_lo, hf), KD)

            def stay_busy(key, w, n):
                b, ps = begin(key)
                for k in range(n):
                    ins = nc.tensor.matmul(ps[:], w[:, 0:P], w[:, 0:HT], start=True, stop=True)
                end(ins, b)
            pe.wait_ge(wa_hi_done, 1)
            stay_busy(("busy", 0), wa_hi[:, 0].rearrange("p k n -> p (k n)"), 7)
            side("right", 0, 0)
            mean_square(("ms", 1), 1, 1)
            pe.wait_ge(rinv_done, 2)
            spread(("rb", 1), 1)
            side("left", 1, 0)
            side("right", 0, 1)

            def gates(hf):
                pe.wait_ge(u_hi_done, KH * (hf + 1))
                pe.wait_ge(u_lo_done, KH * (hf + 1))
                for m in range(KH):
                    for g in range(2):
                        product(("gate", hf, m, g), wa(2 + g)(m), split_of(u_hi, u_lo, hf), KH)

            def out_products(hf):
                pe.wait_ge(y_hi_done, KH * (hf + 1))
                pe.wait_ge(y_lo_done, KH * (hf + 1))
                for dt in range(KD):
                    product(("out", hf, dt), wa(4)(dt), split_of(y_hi, y_lo, hf), KH)

            def mean_square2(hf):
                mean_square(("ms2", hf), hf, hf + 2)

            def spread2(hf):
                pe.wait_ge(rinv_done, hf + 3)
                spread(("rb2", hf), hf)
            wa_ready(3)
            gates(0)
            side("left", 1, 1)
            gates(1)
            pe.wait_ge(wmod2_in, 16)
            modulation("mod_b", range(2 * GA, 2 * GB))
            wa_ready(4)
            stay_busy(("busy", 3), wa_hi[:, 0].rearrange("p k n -> p (k n)"), 12)
            out_products(0)
            mean_square2(0)
            spread2(0)
            pe.wait_ge(wmod3_in, 16)
            for g in range(2):
                b, ps = begin(("gb", g))
                for bb in range(2):
                    for k in range(KD):
                        ins = nc.tensor.matmul(ps[:, bb * D:(bb + 1) * D], cT[:, k, 2 * g + bb:2 * g + bb + 1].to_broadcast([P, P]),
                                               wmod_gb[:, k, :], start=(k == 0), stop=(k == KD - 1))
                end(ins, b)
            pe.wait_ge(ffn_in, 16 * 3)
            transposes("b1", lambda j: rows_e[0:E * KE, :], 1, E * KE)
            wm_ready(3)

            def up(hf, m):
                pe.wait_ge(n_hi_done, KD * (hf + 3))
                pe.wait_ge(n_lo_done, KD * (hf + 3))
                product(("up1", hf, m), wm(0, KD)(m), split_of(n_hi, n_lo, hf), KD)
                product(("up2", hf, m), wm(1, KD)(m), split_of(n_hi, n_lo, hf), KD)

            def down(hf, dts=range(KD)):
                pe.wait_ge(v_hi_done, KF * (hf + 1))
                pe.wait_ge(v_lo_done, KF * (hf + 1))
                for dt in dts:
                    product(("down", hf, dt), wm(2, KF)(dt), split_of(v_hi, v_lo, hf), KF)

            def to_tokens(key, hf, src):
                for p in range(2):
                    b, ps = begin((key, hf, p))
                    for q in range(2):
                        for dt in range(KD):
                            t = hf * TH + 2 * p + q
                            ins = nc.tensor.transpose(ps[:, q * D + dt * P:q * D + (dt + 1) * P], src[:, dt, t * P:(t + 1) * P], ident[:])
                    end(ins, b)

            def x2_to_tokens(hf):
                pe.wait_ge(x2_done, KD * (hf + 1))
                to_tokens("x2t", hf, xT)

            def xhat2_blocks(hf):
                pe.wait_ge(xhat_done, hf + 3)
                for dt in range(KD):
                    transposes(("xh2", hf, dt), lambda j: xhat2[:, j, dt * P:(dt + 1) * P], TH, P)

            def logits(hf):
                b, ps = begin(("logits", hf))
                for dt in range(KD):
                    until_drained(("xh2", hf, dt), 2)
                    for j in range(TH):
                        t = hf * TH + j
                        ins = nc.tensor.matmul(ps[:, j * E:(j + 1) * E], hT[:, dt, t * P:(t + 1) * P], gate_w[:, dt, :],
                                               start=(dt == 0 and j == 0), stop=(dt == KD - 1 and j == TH - 1))
                end(ins, b)

            def places(hf):
                pe.wait_ge(consts2_done, 3)
                pe.wait_ge(sel_done, hf + 1)
                sel = sel_16
                b, ps = begin(("places", hf))
                t0 = hf * TH
                nc.tensor.matmul(ps[:, 0:TH * E], earlier[:], sel[:, t0:t0 + TH, :].rearrange("p t e -> p (t e)"), start=True, stop=False)
                nc.tensor.matmul(ps[:, TH * E:(TH + 1) * E], all_ones[:], sel[:, t0 + TH - 1, :], start=False, stop=False)
                for t in range(t0 + TH - 1):
                    a = max(t + 1 - t0, 0)
                    n = TH + 1 - a
                    ins = nc.tensor.matmul(ps[:, a * E:(a + n) * E].rearrange("p (t e) -> p t e", e=E), all_ones[:],
                                           sel[:, t:t + 1, :].to_broadcast([P, n, E]), start=False, stop=(t == t0 + TH - 2))
                end(ins, b)

            def turn_weights(hf):
                pe.wait_ge(top_done, hf + 1)
                b, ps = begin(("cwT", hf))
                for j in range(TH):
                    ins = nc.tensor.transpose(ps[0:E, j * P:(j + 1) * P], rt[:, 5, hf * TH + j, :], ident[:])
                end(ins, b)

            def second_biases(hf):
                until_drained(("cwT", hf))
                for p in range(2):
                    b, ps = begin(("b2", hf, p))
                    for q in range(2):
                        t = hf * TH + 2 * p + q
                        ins = nc.tensor.matmul(ps[:, q * D:(q + 1) * D], cwT[0:E, t * P:(t + 1) * P], b2_row[0:E, :], start=True, stop=True)
                    end(ins, b)

            up(0, 0)
            up(0, 1)
            out_products(1)
            up(0, 2)
            x_blocks("xr", 0, x_tok)
            mean_square2(1)
            up(0, 3)
            spread2(1)
            up(0, 4)
            x_blocks("xr", 1, x_tok)
            up(0, 5)
            up(1, 0)
            down(0)
            up(1, 1)
            up(1, 2)
            x2_to_tokens(0)
            up(1, 3)
            up(1, 4)
            xhat2_blocks(0)
            up(1, 5)
            logits(0)
            to_tokens("h2t", 0, hT)
            down(1, [0])
            places(0)
            down(1, [1])
            turn_weights(0)
            x2_to_tokens(1)
            second_biases(0)
            stay_busy(("busy", 1), wm_hi[:, 2], 6)
            xhat2_blocks(1)
            logits(1)
            to_tokens("h2t", 1, hT)
            places(1)
            turn_weights(1)
            second_biases(1)
            stay_busy(("busy", 2), wm_hi[:, 2], 16)

            def all_experts():
                pe.wait_ge(h2_hi, NH * KD)
                pe.wait_ge(h2_lo, NH * KD)
                with pe.Fori(0, E) as e:
                    pe.wait_ge(e1_hi_done, e + 1)
                    pe.wait_ge(e1_lo_done, e + 1)
                    for n in range(NH * KE):
                        hf, f = n // KE, n % KE
                        b, _, need = order.at[("s1", n % 4)]
                        pe.wait_ge(drained[b], e * (NH * KE // 4) + need + n // 4)
                        for c in range(KD):
                            for t, (l, r) in enumerate(three([x[:, c, f * P:(f + 1) * P] for x in (e1_hi, e1_lo)], split_of(n_hi, n_lo, hf)(c))):
                                ins = nc.tensor.matmul(bank[b][:], l, r, start=(c == 0 and t == 0), stop=(c == KD - 1 and t == 2))
                        end(ins, b)
                    pe.wait_ge(e2_hi_done, e + 1)
                    pe.wait_ge(e2_lo_done, e + 1)
                    for t8 in range(TT):
                        hf = t8 // TH
                        if t8 % TH == 0:
                            pe.wait_ge(eg_hi_done, e * NH * KE + (hf + 1) * KE)
                            pe.wait_ge(eg_lo_done, e * NH * KE + (hf + 1) * KE)
                        b, _, need = order.at[("rest", t8 % 4)]
                        pe.wait_ge(drained[b], e * (TT // 4) + need + t8 // 4)
                        ts_ = slice(t8 * P, (t8 + 1) * P)
                        for c in range(KE):
                            for t, (l, r) in enumerate(three((g_hi[:, c, ts_], g_lo[:, c, ts_]), (e2_hi[:, c, :], e2_lo[:, c, :]))):
                                ins = nc.tensor.matmul(bank[b][:, 0:D], l, r, start=(c == 0 and t == 0), stop=(c == KE - 1 and t == 2))
                        end(ins, b)

            slot_tiles = [(k, P) for k in range(ST - 1)] + [(ST - 1, LAST)]

            def turn(s):
                for dt in range(KD):
                    for k, n in slot_tiles:
                        ins = nc.tensor.transpose(bank[4 + dt][:, k * P:k * P + n], xe_tok[s][0:n, k, dt * P:(dt + 1) * P], ident[0:n, 0:n])
                    end(ins, 4 + dt)

            def expert(i, s, last):
                e = i * 2 + s
                pe.wait_ge(w1_hi_done, e + 1)
                pe.wait_ge(w1_lo_done, e + 1)
                pe.wait_ge(xe_hi_done, e * KD + KD)
                pe.wait_ge(xe_lo_done, e * KD + KD)
                for f in range(KE):
                    b, _, need = order.at[("s1", f % 4)]
                    pe.wait_ge(drained[b], e * (KE // 4) + need + f // 4)
                    for c in range(KD):
                        for t, (l, r) in enumerate(three([w[s][:, c, f * P:(f + 1) * P] for w in (w1_hi, w1_lo)], (xe_hi[s][:, c, :], xe_lo[s][:, c, :]))):
                            ins = nc.tensor.matmul(bank[b][:, 0:CAP], l, r, start=(c == 0 and t == 0), stop=(c == KD - 1 and t == 2))
                    end(ins, b)
                if not last:
                    pe.wait_ge(xe_in[1 - s], i * 32 + (32 if s == 0 else 64))
                    turn(1 - s)
                pe.wait_ge(w2_hi_done, e + 1)
                pe.wait_ge(w2_lo_done, e + 1)
                for k, n in slot_tiles:
                    b, _, need = order.at[("rest", 2 + k % 2)]
                    per = 1 if k % 2 else 2
                    pe.wait_ge(drained[b], e * per + need + k // 2)
                    for c in range(KE):
                        if k == 0:
                            pe.wait_ge(own_lo_done, e * KE + c + 1)
                        for t, (l, r) in enumerate(three([g[:, c, k * P:k * P + n] for g in (own_hi, own_lo)], (w2_hi[s][:, c, :], w2_lo[s][:, c, :]))):
                            ins = nc.tensor.matmul(bank[b][0:n, 0:D], l, r, start=(c == 0 and t == 0), stop=(c == KE - 1 and t == 2))
                    end(ins, b)

            ov = overflowed(pe)
            with pe.If(ov == 0):
                for j in range(2):
                    b, _, need = order.at[("rest", j)]
                    pe.wait_ge(drained[b], need)
                pe.wait_ge(xe_in[0], 32)
                turn(0)
                with pe.Fori(0, E // 2 - 1) as i:
                    expert(i, 0, False)
                    expert(i, 1, False)
                expert(E // 2 - 1, 0, False)
                expert(E // 2 - 1, 1, True)
            with pe.Else():
                all_experts()

        @block.scalar
        def _(act):
            def full(key):
                b, n, _ = order.at[key]
                act.wait_ge(filled[b], n)
                return b, bank[b]

            def until_drained(key, times=1):
                b, _, before_ = order.at[key]
                act.wait_ge(drained[b], before_ + times)

            hs = [slice(h * HT, (h + 1) * HT) for h in range(NH)]
            act.dma_start(c_row[0:B, :], I["L0_c"]).then_inc(c_in, 16)
            act.dma_start(wmod[:, :, 0:2 * D], packed(I["L0_wmod"])[:, :, 0:2 * D]).then_inc(wmod_in, 16)
            act.wait_ge(consts_done, 2)
            act.wait_ge(c_in, 16)
            nc.scalar.activation(c_row[0:B, :], c_row[0:B, :], ACT.Silu).then_inc(silu_done, 1)

            def a_hi(n):
                act.wait_ge(a_in[n], 16)
                nc.scalar.activation(wa_hi[:, n], raw_a[:, n], ACT.Copy).then_inc(wa_hi_done, 1)

            def m_hi(n):
                act.wait_ge(m_in[n], 16)
                nc.scalar.activation(wm_hi[:, n], raw_m[:, n], ACT.Copy).then_inc(wm_hi_done, 1)

            def ln_root(n):
                hf = (n - 1) % NH
                act.wait_ge(mv_done, n)
                nc.scalar.activation(std[:, hf * TH:(hf + 1) * TH], mv[:, hf * TH:(hf + 1) * TH, 1], ACT.Sqrt,
                                     bias=eps_ln).then_inc(std_done, 1)

            def squares(hf, key, times):
                for dt in range(KD):
                    until_drained((key, hf, dt), times)
                    nc.scalar.activation(square[:, dt, hs[hf]], hT[:, dt, hs[hf]], ACT.Square).then_inc(square_done, 1)

            def mean_root(key, hf):
                b, ps = full(key)
                nc.scalar.activation(rms[:, hf, :], ps[:, 0:TH], ACT.Sqrt, bias=eps_rms, scale=1.0 / D).then_inc(drained[b], 1)

            def hi_of_n(hf, key):
                for dt in range(KD):
                    until_drained(key, dt + 1)
                    nc.scalar.activation(n_hi[:, dt, hs[hf]], xn[:, dt, hs[hf]], ACT.Copy).then_inc(n_hi_done, 1)

            ln_root(1)
            load_vectors(act, names[0::2], vec_in)
            act.dma_start(rows_e[0:E * KE, :], I["L0_ffn_b1"].rearrange("e (k p) -> (e k) p", p=P)).then_inc(ffn_in, 16)
            act.dma_start(gate_w[:], packed(I["L0_ffn_gate_w"])).then_inc(ffn_in, 16)
            act.dma_start(b2_row[0:E, :], I["L0_ffn_b2"]).then_inc(ffn_in, 16)
            squares(0, "xh", 2)
            ln_root(2)
            mean_root(("ms", 0), 0)
            a_hi(0)
            hi_of_n(0, ("rb", 0))
            squares(1, "xh", 2)
            a_hi(1)
            a_hi(2)
            a_hi(3)
            until_drained("vec")
            act.wait_ge(lru_done, 1)

            def right(hf, m):
                n = hf * KH + m
                b, ps = full(("right", hf, m))
                nc.scalar.activation(rbuf[:, n, :, PAD:], ps[:].rearrange("p (b s) -> p b s", b=BH), ACT.Identity,
                                     bias=C("right_b", m)).then_inc(drained[b], 1)
                nc.scalar.activation(u[:, m, hs[hf]], ps[:], ACT.Identity, bias=lru[:, 7, m:m + 1],
                                     scale=C("conv_w", PAD * KH + m)).then_inc(drained[b], 1)

            def u_hi_of(n):
                hf, m = n // KH, n % KH
                act.wait_ge(conv_done, n + 1)
                nc.scalar.activation(u_hi[:, m, hs[hf]], u[:, m, hs[hf]], ACT.Copy).then_inc(u_hi_done, 1)

            def left(hf):
                for m in range(KH):
                    b, ps = full(("left", hf, m))
                    nc.scalar.activation(gel[:, m, hs[hf]], ps[:], ACT.Gelu, bias=C("left_b", m)).then_inc(drained[b], 1)

            def gate_functions(hf, m):
                for g, bias in enumerate(("ga_b", "gx_b")):
                    b, ps = full(("gate", hf, m, g))
                    nc.scalar.activation(tmp[:, 4 * g + hf * KH + m, :], ps[:], ACT.Sigmoid, bias=C(bias, m)).then_inc(drained[b], 1)

            def decays(hf):
                for k in range(hf * KH, (hf + 1) * KH):
                    m = k % KH
                    until_drained(("gate", hf, m, 0))
                    nc.scalar.activation(tmp[:, 8 + k, :], tmp[:, k, :], ACT.Exp, scale=lru[:, 5, m:m + 1]).then_inc(lru_out, 1)
                    act.wait_ge(lru_out, 2 * k + 1)
                    nc.scalar.activation(tmp[:, k, :], tmp[:, k, :], ACT.Tanh, scale=lru[:, 6, m:m + 1]).then_inc(lru_out, 1)

            def roots(hf):
                for k in range(hf * KH, (hf + 1) * KH):
                    act.wait_ge(lru_out, 2 * k + 2)
                    nc.scalar.activation(tmp[:, k, :], tmp[:, k, :], ACT.Sqrt).then_inc(root_out, 1)

            def keep_x(hf):
                for dt in range(KD):
                    b, ps = full(("xr", hf, dt))
                    nc.scalar.activation(xT[:, dt, hs[hf]], ps[:], ACT.Copy).then_inc(drained[b], 1)

            right(0, 0)
            right(0, 1)
            mean_root(("ms", 1), 1)
            u_hi_of(0)
            a_hi(4)
            u_hi_of(1)
            hi_of_n(1, ("rb", 1))
            left(0)
            right(1, 0)
            right(1, 1)
            m_hi(2)
            act.wait_ge(abs_done, 1)
            nc.scalar.activation(lru[:, 1, :], lru[:, 1, :], ACT.Sigmoid).then_inc(abs_done, 1)
            gate_functions(0, 0)
            u_hi_of(2)
            gate_functions(0, 1)
            u_hi_of(3)
            act.wait_ge(lru_done, 2)
            decays(0)
            roots(0)
            left(1)
            m_hi(0)
            m_hi(1)
            for m in range(KH):
                gate_functions(1, m)
            decays(1)
            squares(0, "out", 1)
            roots(1)
            mean_root(("ms2", 0), 0)
            hi_of_n(0, ("rb2", 0))
            act.wait_ge(y_done, NH * KH)

            def v_hi_of(n):
                until_drained(("up2", n // KF, n % KF))
                nc.scalar.activation(v_hi[:, n % KF, hs[n // KF]], tmp[:, 4 + n % 4, :], ACT.Copy).then_inc(v_hi_done, 1)
            def up_gelu(n):
                b, ps = full(("up1", n // KF, n % KF))
                if n >= 4:
                    until_drained(("up2", (n - 4) // KF, (n - 4) % KF))
                nc.scalar.activation(tmp[:, n % 4, :], ps[:], ACT.Gelu, bias=C("up1_b", n % KF)).then_inc(drained[b], 1)
                if n >= 1:
                    v_hi_of(n - 1)

            def keep_x2(hf):
                for p in range(2):
                    until_drained(("x2t", hf, p))
                    b, ps = full(("x2t", hf, p))
                    nc.scalar.activation(x2_tok[:, hf * TH + 2 * p:hf * TH + 2 * p + 2, :], ps[:].rearrange("p (q d) -> p q d", q=2),
                                         ACT.Copy).then_inc(drained[b], 1)

            def keep_h2(hf):
                for p in range(2):
                    b, ps = full(("h2t", hf, p))
                    nc.scalar.activation(h2_tok[:, p, hf, :, :], ps[:].rearrange("p (q d) -> p q d", q=2), ACT.Copy).then_inc(drained[b], 1)

            def numerators(hf):
                ts = slice(hf * TH, (hf + 1) * TH)
                until_drained(("logits", hf), 2)
                nc.scalar.activation(rt[:, 1, ts, :], rt[:, 0, ts, :], ACT.Exp).then_inc(exp_done, 1)

            def keep_weights(hf):
                b, ps = full(("cwT", hf))
                nc.scalar.activation(cwT[0:E, hs[hf]], ps[0:E, :], ACT.Copy).then_inc(drained[b], 1)

            def keep_biases(hf):
                for p in range(2):
                    b, ps = full(("b2", hf, p))
                    nc.scalar.activation(biases[:, hf * TH + 2 * p:hf * TH + 2 * p + 2, :], ps[:].rearrange("p (q d) -> p q d", q=2),
                                         ACT.Copy).then_inc(drained[b], 1)
            for n in range(NH * KF):
                up_gelu(n)
                if n == 1:
                    squares(1, "out", 1)
                if n == 2:
                    keep_x(0)
                    mean_root(("ms2", 1), 1)
                if n == 4:
                    hi_of_n(1, ("rb2", 1))
                    keep_x(1)
                if n == KF + 3:
                    ln_root(3)
                if n == KF + 4:
                    keep_x2(0)
            v_hi_of(NH * KF - 1)
            numerators(0)
            keep_h2(0)
            act.wait_ge(raw1_in, 16)
            nc.scalar.activation(w1_hi[0][:], e_raw1[:].rearrange("p (k n) -> p k n", k=KD), ACT.Copy).then_inc(w1_hi_done, 1)
            act.wait_ge(raw2_in, 16)
            nc.scalar.activation(w2_hi[0][:], e_raw2[:].rearrange("p (k n) -> p k n", k=KE), ACT.Copy).then_inc(w2_hi_done, 1)
            keep_weights(0)
            ln_root(4)
            keep_biases(0)
            keep_x2(1)
            numerators(1)
            keep_h2(1)
            keep_weights(1)
            keep_biases(1)

            def all_experts():
                act.wait_ge(w2_lo_done, 1)
                b, n, _ = order.at[("busy", 2)]
                act.wait_ge(filled[b], n)
                for hf in range(NH):
                    for dt in range(KD):
                        nc.scalar.activation(n_hi[:, dt, hs[hf]], hT[:, dt, hs[hf]], ACT.Copy).then_inc(h2_hi, 1)
                act.wait_ge(rest_done, TT // 2)
                with act.Fori(0, E) as e:
                    act.wait_ge(raw1_in, e * 16 + 48)
                    nc.scalar.activation(e1_hi[:], e_raw1[:].rearrange("p (k n) -> p k n", k=KD), ACT.Copy).then_inc(e1_hi_done, 1)
                    nc.scalar.activation(b1_now[:], b1c[:, bass.ds(e * KE, KE)], ACT.Copy).then_inc(bias_done, 1)
                    act.wait_ge(bias_done, e + 1)
                    for n in range(NH * KE):
                        hf, f = n // KE, n % KE
                        b, base, before_ = order.at[("s1", n % 4)]
                        act.wait_ge(filled[b], e * (NH * KE // 4) + base + n // 4 + 1)
                        act.wait_ge(g_free, e * NH * KE + n + 1)
                        nc.scalar.activation(g_raw[:, n % 4, :], bank[b][:], ACT.Gelu,
                                             bias=b1_now[:, f:f + 1]).then_inc(drained[b], 1)
                        act.wait_ge(drained[b], e * (NH * KE // 4) + before_ + n // 4 + 1)
                        nc.scalar.activation(g_hi[:, f, hs[hf]], g_raw[:, n % 4, :], ACT.Copy).then_inc(eg_hi_done, 1)
                        if n == 3:
                            act.wait_ge(raw2_in, e * 16 + 48)
                            nc.scalar.activation(e2_hi[:], e_raw2[:].rearrange("p (k n) -> p k n", k=KE), ACT.Copy).then_inc(e2_hi_done, 1)

            def x_hi(e, s):
                for dt in range(KD):
                    b, base, _ = order.at[("rest", dt)]
                    act.wait_ge(filled[b], e + base + 1)
                    nc.scalar.activation(xe_hi[s][:, dt, :], bank[b][:, 0:CAP], ACT.Copy).then_inc(xe_hi_done, 1)

            def expert(i, s, last):
                e = i * 2 + s
                act.wait_ge(bias_done, e + 1)
                for f in range(KE):
                    b, base, _ = order.at[("s1", f % 4)]
                    act.wait_ge(filled[b], e * (KE // 4) + base + f // 4 + 1)
                    if f >= 4:
                        act.wait_ge(own_lo_done, e * KE + f - 3)
                    nc.scalar.activation(own_raw[:, f % 4, :], bank[b][:, 0:CAP], ACT.Gelu, bias=b1_own[:, s, f:f + 1]).then_inc(drained[b], 1)
                    if f == 1 and not last:
                        act.wait_ge(raw1_in, e * 16 + 32)
                        nc.scalar.activation(w1_hi[1 - s][:], e_raw1[:].rearrange("p (k n) -> p k n", k=KD), ACT.Copy).then_inc(w1_hi_done, 1)
                if not last:
                    x_hi(e + 1, 1 - s)
                    act.wait_ge(raw2_in, e * 16 + 32)
                    nc.scalar.activation(w2_hi[1 - s][:], e_raw2[:].rearrange("p (k n) -> p k n", k=KE), ACT.Copy).then_inc(w2_hi_done, 1)

            ov = overflowed(act)
            with act.If(ov == 0):
                x_hi(0, 0)
                with act.Fori(0, E // 2 - 1) as i:
                    expert(i, 0, False)
                    expert(i, 1, False)
                expert(E // 2 - 1, 0, False)
                expert(E // 2 - 1, 1, True)
            with act.Else():
                all_experts()

        @block.vector
        def _(dve):
            st = Steps(dve, dve_step)

            def full(key):
                b, n, _ = order.at[key]
                dve.wait_ge(filled[b], n)
                return b, bank[b]

            def until_drained(key, times=1):
                b, _, before_ = order.at[key]
                dve.wait_ge(drained[b], before_ + times)

            hs = [slice(h * HT, (h + 1) * HT) for h in range(NH)]
            nc.vector.memset(small[:, 0:1], 1.0).then_inc(consts_done, 1)
            nc.vector.memset(small[:, 1:2], 1e-5)
            nc.vector.memset(small[:, 2:3], 1e-8).then_inc(consts_done, 1)
            pads = st.mark(nc.vector.memset(rbuf[:, :, :, 0:PAD], 0.0))
            for e in range(E):
                st.mark(nc.vector.memset(unused_slots[:, e:e + 1], float(e * (T - CAP))))
                slot_base_ready = st.mark(nc.vector.memset(slot_base[:, e:e + 1], float(e * T + 1)))
            dve.sem_inc(g_free, 4)
            for s in range(2):
                dve.sem_inc(y_out[s], 32)

            def ln_stats(tile):
                for j, src in tile:
                    last = nc.vector.bn_stats(stat[:, j, :], src)
                st.link(last)
                for j, _ in tile:
                    last = nc.vector.bn_aggr(mv[:, j, :], stat[:, j, :])
                last.then_inc(mv_done, 1)

            def ln_apply(tile, dst, n, empties=None, first=0):
                hf = (n - 1) % NH
                dve.wait_ge(std_done, n)
                st.link(nc.vector.reciprocal(rstd[:, hf * TH:(hf + 1) * TH], std[:, hf * TH:(hf + 1) * TH]))
                for k, (j, src) in enumerate(tile):
                    last = nc.vector.tensor_scalar(dst[:, j - first, :], src, mv[:, j, 0:1], rstd[:, j:j + 1], ALU.subtract, ALU.mult)
                    if empties and k % 2 == 1:
                        last.then_inc(drained[empties[k // 2]], 1)
                return last

            def x_tiles(hf):
                return [(j, x_tok[:, j, :]) for j in range(hf * TH, (hf + 1) * TH)]

            dve.wait_ge(x_in[0], 16)
            ln_stats(x_tiles(0))
            b, ps = full("cT")
            nc.vector.tensor_copy(cT[:], ps[:, 0:KD * B].rearrange("p (k b) -> p k b", k=KD)).then_inc(drained[b], 1)
            ln_apply(x_tiles(0), xhat, 1).then_inc(xhat_done, 1)
            b, ps = full("mod_a")
            nc.vector.tensor_copy(mod[:, 0:2 * KD, :], ps[:, 0:2 * KD * B].rearrange("p (j b) -> p j b", b=B)).then_inc(drained[b], 1)
            until_drained("mod_a")
            scales = st.mark(nc.vector.tensor_scalar(mod[:, 2 * CA:2 * CA + 2, :], mod[:, 2 * CA:2 * CA + 2, :], 1.0, None, ALU.add))
            st.need(scales)

            def modulate(key, hf, scale, shift):
                for dt in range(KD):
                    b, ps = full((key, hf, dt))
                    for q in range(BH):
                        bb = hf * BH + q
                        nc.vector.tensor_scalar(hT[:, dt, bb * S:(bb + 1) * S], ps[:, q * S:(q + 1) * S],
                                                M(scale, dt, bb), M(shift, dt, bb), ALU.mult, ALU.add).then_inc(drained[b], 1)

            modulate("xh", 0, CA, SA)
            dve.wait_ge(x_in[1], 16)
            ln_stats(x_tiles(1))
            b, ps = full("vec")
            nc.vector.tensor_copy(cols[:], ps[:, 0:NV]).then_inc(drained[b], 1)

            def rms_inverse(key, hf, n):
                until_drained(key)
                nc.vector.reciprocal(rinv[:, hf, :], rms[:, hf, :]).then_inc(rinv_done, 1)

            def rms_apply(key, hf, src, w):
                b, ps = full(key)
                for dt in range(KD):
                    until_drained((src[0], hf, dt), src[1])
                for dt in range(KD):
                    ins = nc.vector.scalar_tensor_tensor(out=xn[:, dt, hs[hf]], in0=hT[:, dt, hs[hf]], scalar=C(w, dt), in1=ps[:],
                                                         op0=ALU.mult, op1=ALU.mult)
                    ins.then_inc(drained[b], 1)
                until_drained(key, 2)

            def rms_lo(key, hf, n):
                b, _, _ = order.at[key]
                for dt in range(KD):
                    dve.wait_ge(n_hi_done, KD * (n - 1) + dt + 1)
                    ins = nc.vector.tensor_tensor(n_lo[:, dt, hs[hf]], xn[:, dt, hs[hf]], n_hi[:, dt, hs[hf]].bitcast(F32), ALU.subtract)
                    ins.then_inc(n_lo_done, 1)

            rms_inverse(("ms", 0), 0, 1)
            ln_apply(x_tiles(1), xhat, 2).then_inc(xhat_done, 1)
            until_drained("vec")
            rms_apply(("rb", 0), 0, ("xh", 2), "norm1_w")
            modulate("xh", 1, CA, SA)
            rms_lo(("rb", 0), 0, 1)
            st.link(nc.vector.tensor_tensor(lru[:, 0, :], cols[:, row["right_b"]:row["right_b"] + KH],
                                            cols[:, row["conv_w"] + PAD * KH:row["conv_w"] + TAPS * KH], ALU.mult))
            nc.vector.tensor_tensor(lru[:, 7, :], lru[:, 0, :], cols[:, row["conv_b"]:row["conv_b"] + KH], ALU.add).then_inc(lru_done, 1)
            a_par = cols[:, row["a_param"]:row["a_param"] + KH]
            st.link(nc.vector.tensor_scalar(lru[:, 1, :], a_par, -1.0, None, ALU.mult))
            nc.vector.tensor_tensor(lru[:, 1, :], lru[:, 1, :], a_par, ALU.min).then_inc(abs_done, 1)
            def conv(n):
                hf, m = n // KH, n % KH
                until_drained(("right", hf, m), 2)
                for k in range(PAD):
                    ins = nc.vector.scalar_tensor_tensor(
                        out=u[:, m, hs[hf]].rearrange("p (b s) -> p b s", b=BH), in0=rbuf[:, n, :, k:k + S],
                        scalar=C("conv_w", k * KH + m), in1=u[:, m, hs[hf]].rearrange("p (b s) -> p b s", b=BH),
                        op0=ALU.mult, op1=ALU.add)
                    if k < PAD - 1:
                        st.link(ins)
                ins.then_inc(conv_done, 1)

            def softplus():
                dve.wait_ge(abs_done, 2)
                st.link(nc.vector.tensor_scalar(lru[:, 2, :], lru[:, 1, :], -1.0, 2.0, ALU.mult, ALU.add))
                st.link(nc.vector.reciprocal(lru[:, 2, :], lru[:, 2, :]))
                st.link(nc.vector.tensor_tensor(lru[:, 2, :], lru[:, 2, :], lru[:, 1, :], ALU.mult))
                st.link(nc.vector.tensor_tensor(lru[:, 3, :], lru[:, 2, :], lru[:, 2, :], ALU.mult))
                SERIES = 9
                st.link(nc.vector.tensor_scalar(lru[:, 4, :], lru[:, 3, :], 1.0 / (2 * SERIES + 1), None, ALU.mult))
                for k in range(SERIES - 1, 0, -1):
                    st.link(nc.vector.scalar_tensor_tensor(out=lru[:, 4, :], in0=lru[:, 4, :], scalar=1.0 / (2 * k + 1), in1=lru[:, 3, :],
                                                           op0=ALU.add, op1=ALU.mult))
                st.link(nc.vector.scalar_tensor_tensor(out=lru[:, 4, :], in0=lru[:, 4, :], scalar=1.0, in1=lru[:, 2, :], op0=ALU.add, op1=ALU.mult))
                st.link(nc.vector.tensor_scalar(lru[:, 3, :], a_par, 0.0, 0.5, ALU.max, ALU.mult))
                st.link(nc.vector.tensor_tensor(lru[:, 3, :], lru[:, 3, :], lru[:, 4, :], ALU.add))
                st.link(nc.vector.tensor_scalar(lru[:, 5, :], lru[:, 3, :], -16.0, None, ALU.mult))
                nc.vector.tensor_scalar(lru[:, 6, :], lru[:, 3, :], 8.0, None, ALU.mult).then_inc(lru_done, 1)

            st.need(pads)
            for n in range(NH * KH):
                conv(n)
                if n == 0:
                    rms_inverse(("ms", 1), 1, 2)
                if n == 1:
                    rms_apply(("rb", 1), 1, ("xh", 2), "norm1_w")
                    rms_lo(("rb", 1), 1, 2)
            def bounded(g, s1, s2):
                st.mark(nc.vector.tensor_scalar(s1, g, 0.0, 2.0, ALU.is_ge, ALU.mult))
                st.link(nc.vector.tensor_scalar(s2, g, -1.0, None, ALU.mult))
                st.link(nc.vector.tensor_tensor(s2, s2, g, ALU.max))
                st.link(nc.vector.tensor_scalar(s2, s2, 0.25, None, ALU.max))
                st.link(nc.vector.scalar_tensor_tensor(out=g, in0=s1, scalar=-1.0, in1=s2, op0=ALU.add, op1=ALU.mult))
            def bounded_rows(g):
                until_drained(("gb", g // 2))
                bounded(gbb[:, g, :], bound_tmp[:, 0, :], bound_tmp[:, 1, :])


            def u_of(k):
                return u[:, k % KH, hs[k // KH]]

            def inputs(hf):
                dve.wait_ge(u_lo_done, KH * (hf + 1))
                for k in range(hf * KH, (hf + 1) * KH):
                    until_drained(("gate", hf, k % KH, 1))
                    last = st.mark(nc.vector.tensor_tensor(u_of(k), u_of(k), tmp[:, 4 + k, :], ALU.mult))
                return last

            def recur(k):
                dve.wait_ge(root_out, k + 1)
                st.link(nc.vector.scalar_tensor_tensor(out=tmp[:, k, :], in0=tmp[:, 8 + k, :], scalar=1.0, in1=tmp[:, k, :],
                                                       op0=ALU.add, op1=ALU.mult))
                st.link(nc.vector.tensor_tensor(u_of(k), u_of(k), tmp[:, k, :], ALU.mult))
                for q in range(BH):
                    uq = u_of(k)[:, q * S:(q + 1) * S]
                    last = st.mark(nc.vector.tensor_tensor_scan(uq, tmp[:, 8 + k, q * S:(q + 1) * S], uq, 0.0, ALU.mult, ALU.add))
                st.need(last)
                until_drained(("left", k // KH, k % KH))
                nc.vector.tensor_tensor(u_of(k), gel[:, k % KH, hs[k // KH]], u_of(k), ALU.mult).then_inc(y_done, 1)
                dve.wait_ge(y_done, k + 1)
                nc.vector.tensor_copy(y_hi[:, k % KH, hs[k // KH]], u_of(k)).then_inc(y_hi_done, 1)

            def x1_of(hf):
                for dt in range(KD):
                    b, ps = full(("out", hf, dt))
                    nc.vector.scalar_tensor_tensor(out=hT[:, dt, hs[hf]], in0=ps[:], scalar=C("out_b", dt), in1=hT[:, dt, hs[hf]],
                                                   op0=ALU.add, op1=ALU.add).then_inc(drained[b], 1)
            softplus()
            st.need(inputs(0))
            recur(0)
            recur(1)
            b, ps = full("mod_b")
            nc.vector.tensor_copy(mod[:, 2 * GA:2 * GB, :], ps[:, 2 * GA * B:2 * GB * B].rearrange("p (j b) -> p j b", b=B)).then_inc(drained[b], 1)
            until_drained("mod_b")
            st.mark(nc.vector.tensor_scalar(mod[:, 2 * CB:2 * CB + 2, :], mod[:, 2 * CB:2 * CB + 2, :], 1.0, None, ALU.add))

            st.need(inputs(1))
            x1_of(0)
            rms_inverse(("ms2", 0), 0, 3)
            rms_apply(("rb2", 0), 0, ("out", 1), "norm2_w")
            rms_lo(("rb2", 0), 0, 3)
            recur(2)
            recur(3)
            bounded(mod[:, 2 * GA:2 * GA + 2, :], small[:, 8:16].rearrange("p (k b) -> p k b", k=2),
                    small[:, 16:24].rearrange("p (k b) -> p k b", k=2))
            for g in range(2):
                b, ps = full(("gb", g))
                nc.vector.tensor_copy(gbb[:, 2 * g:2 * g + 2, :], ps[:].rearrange("p (b d) -> p b d", b=2)).then_inc(drained[b], 1)
            b, ps = full("b1")
            nc.vector.tensor_copy(b1c[:], ps[:, 0:E * KE]).then_inc(drained[b], 1)

            def v_of(n):
                hf, m = n // KF, n % KF
                until_drained(("up1", hf, m))
                b, ps = full(("up2", hf, m))
                if n >= 4:
                    dve.wait_ge(v_lo_done, n - 3)
                nc.vector.scalar_tensor_tensor(out=tmp[:, 4 + n % 4, :], in0=ps[:], scalar=C("up2_b", m), in1=tmp[:, n % 4, :],
                                               op0=ALU.add, op1=ALU.mult).then_inc(drained[b], 1)

            def x2_of(hf):
                for dt in range(KD):
                    b, ps = full(("down", hf, dt))
                    nc.vector.scalar_tensor_tensor(out=tmp[:, 8 + dt, :], in0=ps[:], scalar=C("down_b", dt), in1=hT[:, dt, hs[hf]],
                                                   op0=ALU.add, op1=ALU.add).then_inc(drained[b], 1)
                    until_drained(("down", hf, dt))
                    for q in range(BH):
                        bb = hf * BH + q
                        xs = xT[:, dt, bb * S:(bb + 1) * S]
                        ins = nc.vector.scalar_tensor_tensor(out=xs, in0=tmp[:, 8 + dt, q * S:(q + 1) * S], scalar=M(GA, dt, bb), in1=xs,
                                                             op0=ALU.mult, op1=ALU.add)
                        ins.then_inc(x2_done if q else x2_half, 1)

            def x2_tiles(hf):
                tiles = []
                for p in range(2):
                    b, ps = full(("x2t", hf, p))
                    tiles += [(hf * TH + 2 * p + q, ps[:, q * D:(q + 1) * D]) for q in range(2)]
                return tiles

            def second_norm(hf):
                tiles = x2_tiles(hf)
                ln_apply(tiles, xhat2, hf + 3, [order.at[("x2t", hf, p)][0] for p in range(2)], first=hf * TH)
                until_drained(("x2t", hf, 0))
                until_drained(("x2t", hf, 1))
                dve.sem_inc(xhat_done, 1)

            def centre(hf):
                ts = slice(hf * TH, (hf + 1) * TH)
                b, ps = full(("logits", hf))
                lg = ps[:, 0:TH * E].rearrange("p (t e) -> p t e", e=E)
                nc.vector.tensor_reduce(big[:, ts], lg, mybir.AxisListType.X, ALU.max).then_inc(drained[b], 1)
                until_drained(("logits", hf))
                nc.vector.tensor_tensor(rt[:, 0, ts, :], lg, across(big[:, ts]), ALU.subtract).then_inc(drained[b], 1)

            big, high, both = small[:, 24:24 + TT], small[:, 40:40 + TT], small[:, 48:48 + TT]

            def across(v):
                return v.rearrange("p (t e) -> p t e", e=1).to_broadcast([P, TH, E])

            def choose(hf):
                ts = slice(hf * TH, (hf + 1) * TH)
                dve.wait_ge(exp_done, hf + 1)
                pe_ = rt[:, 1, ts, :]
                mine = pe_.rearrange("p t (e o) -> p t e o", o=1).to_broadcast([P, TH, E, E])
                other = pe_.rearrange("p t (o e) -> p t o e", o=1).to_broadcast([P, TH, E, E])
                half = TH * E * E
                beats = rank_tmp[:, 0:half].rearrange("p (t e o) -> p t e o", t=TH, e=E)
                ties = rank_tmp[:, half:2 * half].rearrange("p (t e o) -> p t e o", t=TH, e=E)
                st.mark(nc.vector.tensor_tensor(beats, other, mine, ALU.is_gt))
                st.link(nc.vector.tensor_tensor(ties, other, mine, ALU.is_equal))
                dve.wait_ge(ident_done, 3)
                st.link(nc.vector.tensor_tensor(ties, ties, before[:].rearrange("p (t e) o -> p t e o", t=1).to_broadcast([P, TH, E, E]), ALU.mult))
                st.link(nc.vector.tensor_tensor(beats, beats, ties, ALU.add))
                rank = rt[:, 2, ts, :]
                st.link(nc.vector.tensor_reduce(rank, beats, mybir.AxisListType.X, ALU.add))
                sel = rt[:, 6, ts, :]
                nc.vector.tensor_scalar(sel_16[:, ts, :], rank, 2.0, None, ALU.is_lt).then_inc(sel_done, 1)
                st.link(nc.vector.tensor_scalar(sel, rank, 2.0, None, ALU.is_lt))
                st.link(nc.vector.tensor_tensor(rt[:, 3, ts, :], sel, pe_, ALU.mult))
                st.link(nc.vector.tensor_reduce(big[:, ts], rt[:, 3, ts, :], mybir.AxisListType.X, ALU.add))
                st.link(nc.vector.reciprocal(big[:, ts], big[:, ts]))
                nc.vector.tensor_tensor(rt[:, 5, ts, :], rt[:, 3, ts, :], across(big[:, ts]), ALU.mult).then_inc(top_done, 1)

            def slots(hf):
                ts = slice(hf * TH, (hf + 1) * TH)
                b, ps = full(("places", hf))
                if hf == NH - 1:
                    most = small[:, 32:33]
                    st.link(nc.vector.tensor_reduce(most, ps[:, TH * E:(TH + 1) * E], mybir.AxisListType.X, ALU.max))
                    nc.vector.tensor_scalar(overflow[:], most, float(CAP), None, ALU.is_gt).then_inc(overflow_done, 1)
                slot, sel = rt[:, 7, ts, :], rt[:, 6, ts, :]
                st.need(slot_base_ready)
                nc.vector.tensor_tensor(slot, ps[:, 0:TH * E].rearrange("p (t e) -> p t e", e=E),
                                        slot_base[:].rearrange("p (t e) -> p t e", t=1).to_broadcast([P, TH, E]), ALU.add).then_inc(drained[b], 1)
                until_drained(("places", hf))
                st.link(nc.vector.tensor_tensor(slot, slot, sel, ALU.mult))
                st.mark(nc.vector.tensor_reduce(high[:, ts], slot, mybir.AxisListType.X, ALU.max))
                st.link(nc.vector.tensor_reduce(both[:, ts], slot, mybir.AxisListType.X, ALU.add))
                nc.vector.scalar_tensor_tensor(out=slot_a[:, ts], in0=both[:, ts], scalar=-1.0, in1=high[:, ts], op0=ALU.add, op1=ALU.subtract).then_inc(slots_done, 1)
                nc.vector.tensor_scalar(slot_b[:, ts], high[:, ts], -1.0, None, ALU.add).then_inc(slots_done, 1)

            def two_results():
                slot, sel, here = rt[:, 7, :, :], rt[:, 6, :, :], rt[:, 8, :, :]
                wide = lambda v: v.rearrange("p (t e) -> p t e", e=1).to_broadcast([P, TT, E])
                dve.wait_ge(top_done, NH)
                dve.wait_ge(slots_done, 2 * NH)
                for w, is_it in ((w_b, ALU.is_equal), (w_a, ALU.is_lt)):
                    st.link(nc.vector.tensor_tensor(here, slot, wide(high), is_it))
                    st.link(nc.vector.tensor_tensor(here, here, rt[:, 5, :, :], ALU.mult))
                    st.link(nc.vector.tensor_reduce(w[:], here, mybir.AxisListType.X, ALU.add))
                st.link(nc.vector.tensor_tensor(here, slot, unused_slots[:].rearrange("p (t e) -> p t e", t=1).to_broadcast([P, TT, E]), ALU.subtract))
                st.link(nc.vector.tensor_tensor(here, here, sel, ALU.mult))
                st.mark(nc.vector.tensor_reduce(high, here, mybir.AxisListType.X, ALU.max))
                st.link(nc.vector.tensor_reduce(both, here, mybir.AxisListType.X, ALU.add))
                nc.vector.scalar_tensor_tensor(out=row_a[:], in0=both, scalar=-1.0, in1=high, op0=ALU.add, op1=ALU.subtract).then_inc(rows_done, 1)
                nc.vector.tensor_scalar(row_b[:], high, -1.0, None, ALU.add).then_inc(rows_done, 1)

            for n in range(KF + 1):
                v_of(n)
                if n == 1:
                    x1_of(1)
                if n == 2:
                    rms_inverse(("ms2", 1), 1, 4)
                if n == 3:
                    rms_apply(("rb2", 1), 1, ("out", 1), "norm2_w")
                if n == 4:
                    rms_lo(("rb2", 1), 1, 4)
                if n == 5:
                    bounded_rows(0)
            until_drained(("xr", 0, 0))
            until_drained(("xr", 0, 1))
            x2_of(0)
            v_of(KF + 1)
            bounded_rows(1)
            v_of(KF + 2)
            bounded_rows(2)
            ln_stats(x2_tiles(0))
            v_of(KF + 3)
            second_norm(0)
            v_of(KF + 4)
            modulate("xh2", 0, CB, SB)
            v_of(KF + 5)
            bounded_rows(3)
            centre(0)
            choose(0)
            slots(0)
            until_drained(("xr", 1, 0))
            until_drained(("xr", 1, 1))
            x2_of(1)
            ln_stats(x2_tiles(1))
            second_norm(1)
            modulate("xh2", 1, CB, SB)
            centre(1)
            choose(1)
            slots(1)
            for hf in range(NH):
                for k in range(2):
                    p = 2 * hf + k
                    until_drained(("b2", hf, k))
                    until_drained(("h2t", hf, k))
                    until_drained(("x2t", hf, 1), 2)
                    g = gbb[:, 2 * p * P // S:2 * p * P // S + 1, :].to_broadcast([P, 2, D])
                    bits = biases[:, 2 * p:2 * p + 2, :]
                    st.link(nc.vector.tensor_tensor(bits, bits, h2_tok[:, k, hf, :, :], ALU.add))
                    st.link(nc.vector.tensor_tensor(bits, bits, g, ALU.mult))
                    nc.vector.tensor_tensor(x2_tok[:, 2 * p:2 * p + 2, :], x2_tok[:, 2 * p:2 * p + 2, :], bits, ALU.add).then_inc(rest_done, 1)
            two_results()
            dve.wait_ge(rest_done, TT // 2)
            at_branch = st.n
            ov = overflowed(dve)
            with dve.If(ov == 0):
                def times_gb(y, w, gathered, t):
                    dve.wait_ge(gathered[t], 16)
                    st.link(nc.vector.scalar_tensor_tensor(out=y[:, t, :], in0=y[:, t, :], scalar=w[:, t:t + 1],
                                                           in1=gbb[:, t * P // S, :], op0=ALU.mult, op1=ALU.mult))

                def add_a(t):
                    times_gb(y_a, w_a, a_gathered, t)
                    return st.mark(nc.vector.tensor_tensor(x2_tok[:, t, :], x2_tok[:, t, :], y_a[:, t, :], ALU.add))

                def x_lo(e, s):
                    for dt in range(KD):
                        b, base, _ = order.at[("rest", dt)]
                        dve.wait_ge(xe_hi_done, e * KD + dt + 1)
                        nc.vector.tensor_tensor(xe_lo[s][:, dt, :], bank[b][:, 0:CAP], xe_hi[s][:, dt, :].bitcast(F32), ALU.subtract).then_inc(xe_lo_done, 1)

                def expert(i, s, last):
                    e = i * 2 + s
                    nc.vector.tensor_copy(b1_own[:, s, :], b1c[:, bass.ds(e * KE, KE)]).then_inc(bias_done, 1)
                    for f in range(KE):
                        b, _, before_ = order.at[("s1", f % 4)]
                        dve.wait_ge(drained[b], e * (KE // 4) + before_ + f // 4 + 1)
                        nc.vector.tensor_copy(own_hi[:, f, :], own_raw[:, f % 4, :]).then_inc(own_hi_done, 1)
                        dve.wait_ge(own_hi_done, e * KE + f + 1)
                        nc.vector.tensor_tensor(own_lo[:, f, :], own_raw[:, f % 4, :], own_hi[:, f, :].bitcast(F32), ALU.subtract).then_inc(own_lo_done, 1)
                    if not last:
                        x_lo(e + 1, 1 - s)
                    dve.wait_ge(y_out[s], i * 32 + 32)
                    for k in range(ST):
                        n = P if k < ST - 1 else LAST
                        b, base, _ = order.at[("rest", 2 + k % 2)]
                        dve.wait_ge(filled[b], e * (1 if k % 2 else 2) + base + k // 2 + 1)
                        nc.vector.tensor_copy(y_tok[s][0:n, k, :], bank[b][0:n, 0:D]).then_inc(drained[b], 1)
                        if last and k < ST - 1:
                            add_a(2 * k)
                            add_a(2 * k + 1)
                    for j, per in ((2, 2), (3, 1)):
                        b, _, before_ = order.at[("rest", j)]
                        dve.wait_ge(drained[b], e * per + before_ + per)
                    dve.sem_inc(y_made, 1)
                x_lo(0, 0)
                with dve.Fori(0, E // 2 - 1) as i:
                    expert(i, 0, False)
                    expert(i, 1, False)
                expert(E // 2 - 1, 0, False)
                expert(E // 2 - 1, 1, True)
                for t in range(2 * (ST - 1), TT):
                    a_added = add_a(t)
                st.need(a_added)
                for t in range(TT):
                    times_gb(y_b, w_b, b_gathered, t)
                    nc.vector.tensor_tensor(y_b[:, t, :], x2_tok[:, t, :], y_b[:, t, :], ALU.add).then_inc(acc_done, 1)
            with dve.Else():
                st.n = at_branch
                nc.vector.memset(acc[:], 0.0).then_inc(acc_turn, 1)
                for hf in range(NH):
                    for dt in range(KD):
                        dve.wait_ge(h2_hi, hf * KD + dt + 1)
                        nc.vector.tensor_tensor(n_lo[:, dt, hs[hf]], hT[:, dt, hs[hf]], n_hi[:, dt, hs[hf]].bitcast(F32), ALU.subtract).then_inc(h2_lo, 1)
                with dve.Fori(0, E) as e:
                    for n in range(NH * KE):
                        hf, f = n // KE, n % KE
                        dve.wait_ge(eg_hi_done, e * NH * KE + n + 1)
                        nc.vector.tensor_tensor(g_lo[:, f, hs[hf]], g_raw[:, n % 4, :], g_hi[:, f, hs[hf]].bitcast(F32), ALU.subtract).then_inc(eg_lo_done, 1)
                        dve.wait_ge(eg_lo_done, e * NH * KE + n + 1)
                        dve.sem_inc(g_free, 1)
                    for t8 in range(TT):
                        b, base, before_ = order.at[("rest", t8 % 4)]
                        dve.wait_ge(filled[b], e * (TT // 4) + base + t8 // 4 + 1)
                        dve.wait_ge(acc_turn, e * TT + 1)
                        nc.vector.scalar_tensor_tensor(out=acc[:, t8, :], in0=bank[b][:, 0:D], scalar=rt[:, 5, t8, bass.ds(e, 1)],
                                                       in1=acc[:, t8, :], op0=ALU.mult, op1=ALU.add).then_inc(drained[b], 1)
                        dve.wait_ge(drained[b], e * (TT // 4) + before_ + t8 // 4 + 1)
                        dve.sem_inc(acc_turn, 1)
                for t in range(TT):
                    st.link(nc.vector.tensor_tensor(acc[:, t, :], acc[:, t, :], gbb[:, t * P // S, :], ALU.mult))
                    nc.vector.tensor_tensor(acc[:, t, :], acc[:, t, :], x2_tok[:, t, :], ALU.add).then_inc(acc_done, 1)

        @block.gpsimd
        def _(pool):
            hs = [slice(h * HT, (h + 1) * HT) for h in range(NH)]
            load_vectors(pool, names[1::2], vec2_in)
            nc.gpsimd.memset(ident[:], 0.0).then_inc(ident_done, 1)
            pool.wait_ge(ident_done, 1)
            nc.gpsimd.affine_select(out=ident[:], in_=ident[:], compare_op=ALU.not_equal, fill=1.0, base=0,
                                    pattern=[[-1, P]], channel_multiplier=1).then_inc(ident_done, 1)
            nc.gpsimd.memset(all_ones[:], 1.0).then_inc(consts2_done, 1)
            nc.gpsimd.memset(earlier[:], 1.0).then_inc(consts2_done, 1)
            pool.wait_ge(consts2_done, 2)
            nc.gpsimd.affine_select(out=earlier[:], in_=earlier[:], compare_op=ALU.is_gt, fill=0.0, base=0,
                                    pattern=[[1, P]], channel_multiplier=-1).then_inc(consts2_done, 1)
            nc.gpsimd.memset(before[:], 1.0).then_inc(pool_step, 1)
            pool.wait_ge(pool_step, 1)
            nc.gpsimd.affine_select(out=before[:], in_=before[:], compare_op=ALU.is_gt, fill=0.0, base=0,
                                    pattern=[[1, E], [-1, E]], channel_multiplier=0).then_inc(ident_done, 1)

            def until_drained(key, times=1):
                b, _, before_ = order.at[key]
                pool.wait_ge(drained[b], before_ + times)

            def lo(dst, whole, hi, done):
                nc.gpsimd.tensor_tensor(dst, whole, hi.bitcast(F32), ALU.subtract).then_inc(done, 1)

            def a_lo(n):
                pool.wait_ge(wa_hi_done, n + 1)
                lo(wa_lo[:, n], raw_a[:, n], wa_hi[:, n], wa_lo_done)

            def m_lo(n, done):
                pool.wait_ge(wm_hi_done, done)
                lo(wm_lo[:, n], raw_m[:, n], wm_hi[:, n], wm_lo_done)

            def u_rest(n):
                hf, m = n // KH, n % KH
                pool.wait_ge(u_hi_done, n + 1)
                lo(u_lo[:, m, hs[hf]], u[:, m, hs[hf]], u_hi[:, m, hs[hf]], u_lo_done)

            def y_rest(n):
                hf, m = n // KH, n % KH
                pool.wait_ge(y_hi_done, n + 1)
                lo(y_lo[:, m, hs[hf]], u[:, m, hs[hf]], y_hi[:, m, hs[hf]], y_lo_done)
            a_lo(0)
            for n in range(1, 4):
                a_lo(n)
            u_rest(0)
            a_lo(4)
            u_rest(1)
            m_lo(2, 1)
            u_rest(2)
            u_rest(3)
            y_rest(0)
            y_rest(1)
            b, n, _ = order.at["mod_b"]
            pool.wait_ge(filled[b], n)
            m_lo(0, 2)
            m_lo(1, 3)
            y_rest(2)
            y_rest(3)
            for n in range(NH * KF):
                hf, m = n // KF, n % KF
                pool.wait_ge(v_hi_done, n + 1)
                lo(v_lo[:, m, hs[hf]], tmp[:, 4 + n % 4, :], v_hi[:, m, hs[hf]], v_lo_done)
            def w_lo(e, s, which):
                if which == 1:
                    pool.wait_ge(w1_hi_done, e + 1)
                    lo(w1_lo[s][:], e_raw1[:].rearrange("p (k n) -> p k n", k=KD), w1_hi[s][:], w1_lo_done)
                else:
                    pool.wait_ge(w2_hi_done, e + 1)
                    lo(w2_lo[s][:], e_raw2[:].rearrange("p (k n) -> p k n", k=KE), w2_hi[s][:], w2_lo_done)

            def scatter(t, slots_, done):
                nc.gpsimd.indirect_dma_start(x_rows, bass.IndirectOffsetOnAxis(ap=slots_[:, t:t + 1], axis=0), h2_tile(t), None).then_inc(done, 16)

            def gather(t, y, rows_, slots_, done):
                nc.gpsimd.indirect_dma_start(y[:, t, :], None, rows_, bass.IndirectOffsetOnAxis(ap=slots_[:, t:t + 1], axis=0)).then_inc(done, 16)

            def to_experts(hf):
                for p in range(2):
                    until_drained(("h2t", hf, p))
                pool.wait_ge(slots_done, 2 * hf + 1)
                for j in range(TH):
                    scatter(hf * TH + j, slot_a, a_scattered[hf])
                pool.wait_ge(slots_done, 2 * hf + 2)
                for j in range(TH):
                    scatter(hf * TH + j, slot_b, b_scattered[hf])
            w_lo(0, 0, 1)
            pool.wait_ge(rows_filled, 16)
            to_experts(0)
            w_lo(0, 0, 2)
            to_experts(1)
            ov = overflowed(pool)
            with pool.If(ov == 0):
                def expert(i, s):
                    w_lo(i * 2 + s + 1, 1 - s, 1)
                    w_lo(i * 2 + s + 1, 1 - s, 2)
                with pool.Fori(0, E // 2 - 1) as i:
                    expert(i, 0)
                    expert(i, 1)
                expert(E // 2 - 1, 0)
                pool.wait_ge(y_out[0], 32 * (E // 2 + 1))
                pool.wait_ge(y_out[1], 32 * (E // 2))
                pool.wait_ge(rows_done, 2)
                for t in range(TT):
                    gather(t, y_a, y_rows[0:(E - 1) * CAP], row_a, a_gathered[t])
                pool.wait_ge(y_out[1], 32 * (E // 2 + 1))
                for t in range(TT):
                    gather(t, y_b, y_rows, row_b, b_gathered[t])
            with pool.Else():
                b, n, _ = order.at[("busy", 2)]
                pool.wait_ge(filled[b], n)
                with pool.Fori(0, E) as e:
                    pool.wait_ge(e1_hi_done, e + 1)
                    lo(e1_lo[:], e_raw1[:].rearrange("p (k n) -> p k n", k=KD), e1_hi[:], e1_lo_done)
                    pool.wait_ge(e2_hi_done, e + 1)
                    lo(e2_lo[:], e_raw2[:].rearrange("p (k n) -> p k n", k=KE), e2_hi[:], e2_lo_done)


_OUT_SHAPE = (4, 256, 256)


def kernel(**inputs):
    import numpy as np
    import concourse.bacc as bacc
    from concourse.bass_utils import run_bass_kernel_spmd

    nc = bacc.Bacc("TRN2", target_bir_lowering=False, num_devices=1)
    arrays, aps = {}, {}
    for name, a in inputs.items():
        a = np.ascontiguousarray(a)
        arrays[f"in_{name}"] = a
        aps[name] = nc.dram_tensor(f"in_{name}", a.shape, mybir.dt.from_np(a.dtype), kind="ExternalInput").ap()
    out = nc.dram_tensor("out_x", _OUT_SHAPE, F32, kind="ExternalOutput").ap()
    adaln_block(nc, aps, out)
    return run_bass_kernel_spmd(nc, [arrays], core_ids=[0]).results[0]["out_x"]
```
